# Optimizing a Trainium2 kernel written in Bass

```python
import numpy as np
import jax
import jax.numpy as jnp

def _softmax(x, axis=-1):
    return jax.nn.softmax(x, axis=axis)

def _gelu(x):
    return jax.nn.gelu(x, approximate=True)

def _silu(x):
    return jax.nn.silu(x)

def _sigmoid(x):
    return jax.nn.sigmoid(x)

def _layernorm(x, axis=-1, eps=1e-05):
    m = jnp.mean(x, axis=axis, keepdims=True)
    v = jnp.var(x, axis=axis, keepdims=True)
    return (x - m) / jnp.sqrt(v + eps)

def _scatter_add(tgt, idx, src, axis=0):
    return tgt.at[idx].add(src)

def _segment_sum(src, seg, n):
    return jax.ops.segment_sum(src, seg, n)
kernel_name = 'mk_xattn_ffn_d1_seqx_r4_c09d8c'

def setup_inputs(seed: int=0):
    np.random.seed(seed)
    _w = jnp.asarray

    def _rec_inputs():
        import jax
        import jax.numpy as jnp
        _rk = jax.random.key(seed)
        x = 6.313e-05 + 0.9998 * jax.random.normal(jax.random.fold_in(_rk, 1), (8, 100, 256), jnp.float32)
        _lenS = 100 - jax.random.randint(jax.random.fold_in(_rk, 7), (8,), 0, max(1, 100 // 4) + 1, jnp.int32)
        _lenS2 = 361 - jax.random.randint(jax.random.fold_in(_rk, 8), (8,), 0, max(1, 361 // 4) + 1, jnp.int32)
        _ctx_1024P = jax.random.normal(jax.random.fold_in(_rk, 11), (8, 16, 256), jnp.float32)
        _ctx_1024c = jax.random.dirichlet(jax.random.fold_in(_rk, 511), 0.3 * jnp.ones((16,), jnp.float32), (8, 361))
        _ctx_1024t = jnp.einsum('bsk,bkd->bsd', _ctx_1024c, _ctx_1024P)
        _ctx_1024t = _ctx_1024t * jax.lax.rsqrt(jnp.mean(jnp.square(_ctx_1024t)) + 1e-12) * 0.953939
        ctx_1024 = -0.000214406 + 1.00034 * (_ctx_1024t + 0.3 * jax.random.normal(jax.random.fold_in(_rk, 611), (8, 361, 256), jnp.float32))
        return (x, ctx_1024)
    x, ctx_1024 = _rec_inputs()

    def _L0_xattn_setup():
        import jax, jax.numpy as jnp
        import numpy as np
        from jax import lax
        BIG = jnp.float32(1e+30)

        def _pairwise_euclidean(a, b):
            aa = jnp.sum(a * a, axis=-1)[:, None]
            bb = jnp.sum(b * b, axis=-1)[None, :]
            ab = a @ b.T
            return jnp.sqrt(jnp.maximum(aa + bb - 2.0 * ab, 0.0))

        def _dtw_cost(D):
            row0 = jnp.cumsum(D[0])

            def row_step(prev_row, d_row):
                first = d_row[0] + prev_row[0]

                def col_step(left, inp):
                    d_ij, up, diag = inp
                    r = d_ij + jnp.minimum(jnp.minimum(up, left), diag)
                    return (r, r)
                _, rest = lax.scan(col_step, first, (d_row[1:], prev_row[1:], prev_row[:-1]))
                row = jnp.concatenate([first[None], rest])
                return (row, row)
            _, rows = lax.scan(row_step, row0, D[1:])
            return jnp.concatenate([row0[None], rows], axis=0)

        def _backtrack(R, T1, T2):
            L = T1 + T2 - 1

            def step(carry, _):
                i, j, done = carry
                valid = jnp.logical_not(done)
                cd = jnp.where((i > 0) & (j > 0), R[jnp.maximum(i - 1, 0), jnp.maximum(j - 1, 0)], BIG)
                cu = jnp.where(i > 0, R[jnp.maximum(i - 1, 0), j], BIG)
                cl = jnp.where(j > 0, R[i, jnp.maximum(j - 1, 0)], BIG)
                choice = jnp.argmin(jnp.stack([cd, cu, cl]))
                ni = jnp.where(choice <= 1, i - 1, i)
                nj = jnp.where((choice == 0) | (choice == 2), j - 1, j)
                at_origin = (i == 0) & (j == 0)
                ni = jnp.where(at_origin, 0, ni)
                nj = jnp.where(at_origin, 0, nj)
                return ((ni, nj, done | at_origin), (i, j, valid))
            init = (jnp.int32(T1 - 1), jnp.int32(T2 - 1), jnp.bool_(False))
            _, (i_idx, j_idx, valid) = lax.scan(step, init, None, length=L)
            return (i_idx, j_idx, valid)

        def _align_one(small, large):
            T_small, d = small.shape
            T_large = large.shape[0]
            D = _pairwise_euclidean(small, large)
            R = _dtw_cost(D)
            i_idx, j_idx, valid = _backtrack(R, T_small, T_large)
            contrib = small[i_idx] * valid[:, None].astype(small.dtype)
            expanded = jnp.zeros((T_large, d), dtype=small.dtype).at[j_idx].add(contrib)
            return expanded
        key = jax.random.key(seed)
        k1, k2 = jax.random.split(key)
        teacher = jax.random.normal(k1, (16, 100, 256), dtype=jnp.float32)
        student = jax.random.normal(k2, (16, 150, 256), dtype=jnp.float32)
        return {'teacher_features': teacher, 'student_features': student}
    _L0_xattn_all = _L0_xattn_setup()
    _L0_xattn_in = {k: v for k, v in _L0_xattn_all.items() if k in ()}
    del _L0_xattn_all

    def _L0_ffn_setup():
        import jax, jax.numpy as jnp
        import numpy as np
        HIDDEN = 256
        INTER = 1024
        NUM_EXPERTS = 8
        TOP_K = 2
        EPS = 1e-05

        def _layer_norm(x, g, b):
            m = jnp.mean(x, axis=-1, keepdims=True)
            v = jnp.mean(jnp.square(x - m), axis=-1, keepdims=True)
            return (x - m) * jax.lax.rsqrt(v + EPS) * g + b
        key = jax.random.key(seed)
        ks = jax.random.split(key, 8)
        s = 0.02
        return {'x': jax.random.normal(ks[0], (4, 512, HIDDEN), dtype=jnp.float32), 'ln1_g': jnp.ones((HIDDEN,), jnp.float32), 'ln1_b': jnp.zeros((HIDDEN,), jnp.float32), 'attn_w': jax.random.normal(ks[1], (HIDDEN, HIDDEN), jnp.float32) * s, 'ln2_g': jnp.ones((HIDDEN,), jnp.float32), 'ln2_b': jnp.zeros((HIDDEN,), jnp.float32), 'gate_w': jax.random.normal(ks[2], (NUM_EXPERTS, HIDDEN), jnp.float32) * s, 'gate_proj': jax.random.normal(ks[3], (NUM_EXPERTS, INTER, HIDDEN), jnp.float32) * s, 'up_proj': jax.random.normal(ks[4], (NUM_EXPERTS, INTER, HIDDEN), jnp.float32) * s, 'down_proj': jax.random.normal(ks[5], (NUM_EXPERTS, HIDDEN, INTER), jnp.float32) * s}
    _L0_ffn_all = _L0_ffn_setup()
    _L0_ffn_in = {k: v for k, v in _L0_ffn_all.items() if k in ('ln1_g', 'ln1_b', 'attn_w', 'ln2_g', 'ln2_b', 'gate_w', 'gate_proj', 'up_proj', 'down_proj')}
    del _L0_ffn_all
    return {'x': x, 'ctx_1024': ctx_1024, 'L0_ffn_ln1_g': _L0_ffn_in['ln1_g'], 'L0_ffn_ln1_b': _L0_ffn_in['ln1_b'], 'L0_ffn_attn_w': _L0_ffn_in['attn_w'], 'L0_ffn_ln2_g': _L0_ffn_in['ln2_g'], 'L0_ffn_ln2_b': _L0_ffn_in['ln2_b'], 'L0_ffn_gate_w': _L0_ffn_in['gate_w'], 'L0_ffn_gate_proj': _L0_ffn_in['gate_proj'], 'L0_ffn_up_proj': _L0_ffn_in['up_proj'], 'L0_ffn_down_proj': _L0_ffn_in['down_proj']}

def reference(x, ctx_1024, L0_ffn_ln1_g, L0_ffn_ln1_b, L0_ffn_attn_w, L0_ffn_ln2_g, L0_ffn_ln2_b, L0_ffn_gate_w, L0_ffn_gate_proj, L0_ffn_up_proj, L0_ffn_down_proj):
    import jax
    import jax.numpy as jnp

    def _L0_xattn_ref(teacher_features, student_features):
        import jax, jax.numpy as jnp
        import numpy as np
        from jax import lax
        BIG = jnp.float32(1e+30)

        def _pairwise_euclidean(a, b):
            aa = jnp.sum(a * a, axis=-1)[:, None]
            bb = jnp.sum(b * b, axis=-1)[None, :]
            ab = a @ b.T
            return jnp.sqrt(jnp.maximum(aa + bb - 2.0 * ab, 0.0))

        def _dtw_cost(D):
            row0 = jnp.cumsum(D[0])

            def row_step(prev_row, d_row):
                first = d_row[0] + prev_row[0]

                def col_step(left, inp):
                    d_ij, up, diag = inp
                    r = d_ij + jnp.minimum(jnp.minimum(up, left), diag)
                    return (r, r)
                _, rest = lax.scan(col_step, first, (d_row[1:], prev_row[1:], prev_row[:-1]))
                row = jnp.concatenate([first[None], rest])
                return (row, row)
            _, rows = lax.scan(row_step, row0, D[1:])
            return jnp.concatenate([row0[None], rows], axis=0)

        def _backtrack(R, T1, T2):
            L = T1 + T2 - 1

            def step(carry, _):
                i, j, done = carry
                valid = jnp.logical_not(done)
                cd = jnp.where((i > 0) & (j > 0), R[jnp.maximum(i - 1, 0), jnp.maximum(j - 1, 0)], BIG)
                cu = jnp.where(i > 0, R[jnp.maximum(i - 1, 0), j], BIG)
                cl = jnp.where(j > 0, R[i, jnp.maximum(j - 1, 0)], BIG)
                choice = jnp.argmin(jnp.stack([cd, cu, cl]))
                ni = jnp.where(choice <= 1, i - 1, i)
                nj = jnp.where((choice == 0) | (choice == 2), j - 1, j)
                at_origin = (i == 0) & (j == 0)
                ni = jnp.where(at_origin, 0, ni)
                nj = jnp.where(at_origin, 0, nj)
                return ((ni, nj, done | at_origin), (i, j, valid))
            init = (jnp.int32(T1 - 1), jnp.int32(T2 - 1), jnp.bool_(False))
            _, (i_idx, j_idx, valid) = lax.scan(step, init, None, length=L)
            return (i_idx, j_idx, valid)

        def _align_one(small, large):
            T_small, d = small.shape
            T_large = large.shape[0]
            D = _pairwise_euclidean(small, large)
            R = _dtw_cost(D)
            i_idx, j_idx, valid = _backtrack(R, T_small, T_large)
            contrib = small[i_idx] * valid[:, None].astype(small.dtype)
            expanded = jnp.zeros((T_large, d), dtype=small.dtype).at[j_idx].add(contrib)
            return expanded
        return jax.vmap(_align_one)(teacher_features, student_features)

    def _L0_ffn_ref(x, ln1_g, ln1_b, attn_w, ln2_g, ln2_b, gate_w, gate_proj, up_proj, down_proj):
        import jax, jax.numpy as jnp
        import numpy as np
        HIDDEN = 256
        INTER = 1024
        NUM_EXPERTS = 8
        TOP_K = 2
        EPS = 1e-05

        def _layer_norm(x, g, b):
            m = jnp.mean(x, axis=-1, keepdims=True)
            v = jnp.mean(jnp.square(x - m), axis=-1, keepdims=True)
            return (x - m) * jax.lax.rsqrt(v + EPS) * g + b
        B, S, H = x.shape
        h = x + jnp.einsum('bsh,oh->bso', _layer_norm(x, ln1_g, ln1_b), attn_w)
        t = _layer_norm(h, ln2_g, ln2_b).reshape(-1, H)
        T = t.shape[0]
        logits = jnp.einsum('th,eh->te', t, gate_w)
        top_vals, top_idx = jax.lax.top_k(logits, TOP_K)
        rw = jax.nn.softmax(top_vals, axis=-1)
        comb = jnp.zeros((T, NUM_EXPERTS), dtype=t.dtype)
        comb = comb.at[jnp.arange(T)[:, None], top_idx].add(rw)
        out = jnp.zeros_like(t)
        for e in range(NUM_EXPERTS):
            g = jnp.einsum('th,ih->ti', t, gate_proj[e])
            u = jnp.einsum('th,ih->ti', t, up_proj[e])
            oe = jnp.einsum('ti,hi->th', jax.nn.silu(g) * u, down_proj[e])
            out = out + comb[:, e:e + 1] * oe
        return h + out.reshape(B, S, H)
    x = x + _L0_xattn_ref(ctx_1024, _layernorm(x, axis=-1))
    x = x + _L0_ffn_ref(_layernorm(x, axis=-1), L0_ffn_ln1_g, L0_ffn_ln1_b, L0_ffn_attn_w, L0_ffn_ln2_g, L0_ffn_ln2_b, L0_ffn_gate_w, L0_ffn_gate_proj, L0_ffn_up_proj, L0_ffn_down_proj)
    return x

_drawn_inputs = setup_inputs


def setup_inputs(seed=0):
    import zlib

    import numpy as np

    out = dict(_drawn_inputs(seed))
    spreads = {'L0_ffn_ln1_g': (1.0, 0.6),
     'L0_ffn_ln1_b': (0.0, 0.8),
     'L0_ffn_ln2_g': (1.0, 0.6),
     'L0_ffn_ln2_b': (0.0, 0.8)}
    factors = {'L0_ffn_gate_w': 8.0,
     'L0_ffn_gate_proj': 8.0,
     'L0_ffn_up_proj': 8.0,
     'L0_ffn_down_proj': 8.0}
    for name, (base, spread) in spreads.items():
        noise = np.random.default_rng([zlib.crc32(name.encode()), seed]).standard_normal(out[name].shape)
        drawn = base * np.exp(spread * noise) if base else spread * noise
        out[name] = jnp.asarray(drawn.astype(out[name].dtype))
    for name, factor in factors.items():
        out[name] = (out[name] * factor).astype(out[name].dtype)
    return out
```

```python
from contextlib import ExitStack

import concourse.bass as bass
from concourse import mybir

F32 = mybir.dt.float32
BF16 = mybir.dt.bfloat16
U32 = mybir.dt.uint32
ALU = mybir.AluOpType
ACT = mybir.ActivationFunctionType
AX_X = mybir.AxisListType.X

NB = 8
J = 100
NI = 361
H = 256
HC = H // 128
F = 1024
FC = F // 128
NE = 8
BR = 25
KB = 16
CB = 5
NC = 3
CR = CB * BR
LAST = NI - (NC - 1) * CR
W = J + NC * CB - 1
END_K, END_R = (NI - 1) // BR, (NI - 1) % BR
G = 4
BIG = 1e30
EPS = 1e-5
RING = 3
EW = 3 * HC * F


def align_and_route(nc, x, ctx_t, ctx_n, ln, attn_t, gate_t, gate_proj, up_proj, down_proj, out):
    with ExitStack() as stack:
        def sb(name, shape, dt=F32):
            return stack.enter_context(nc.sbuf_tensor(name, shape, dt))

        def sem(name):
            return stack.enter_context(nc.semaphore(name))

        bank = [stack.enter_context(nc.psum_tensor(f"bank{i}", [128, 512], F32)) for i in range(8)]

        rows_out = nc.dram_tensor("distance_rows", (NC * CR, NB, J), F32, kind="Internal").ap()
        rows_back = nc.dram_tensor("path_rows", (NC * CR, NB, J), F32, kind="Internal").ap()

        weights = sb("weights", [128, RING, EW])
        big = sb("big", [128, BR, W])
        cost = sb("cost", [128, W + 1, BR + 1])
        shared = sb("shared", [128, HC * NB * NC * CR])
        trail = sb("trail", [128, W + 1, 2 * BR + 1], BF16)
        stage = sb("stage", [128, NC, NB, J])
        ctxn = sb("ctxn", [128, NC, NB, H])
        xs = sb("xs", [128, NB, H])
        xn = sb("xn", [128, NB, H])
        xT = sb("xT", [128, HC, NB, J])
        attn_w = sb("attn_w", [128, HC, H])
        gate_w = sb("gate_w", [128, HC, NE])
        ln_w = sb("ln_w", [128, 4, HC])
        ident = sb("ident", [128, 128])
        sel = sb("sel", [NB, NB, CR])
        seed = sb("seed", [128, 2 * BR], BF16)
        first = sb("first", [128, 2])
        bn6 = sb("bn6", [128, NB, 6])
        mv = sb("mv", [128, NB, 2])
        std = sb("std", [128, NB])
        rstd = sb("rstd", [128, NB])
        sq = sb("sq", [128, H])
        aa = sb("aa", [128, NC, NB])
        bb = sb("bb", [128, NB])
        bbT = sb("bbT", [NB, J])
        eps = sb("eps", [128, 1])
        best = sb("best", [128, 2, BR])
        step_in = sb("step_in", [128, 2, 2 * BR], BF16)
        top = sb("top", [128, NB, 8])
        logit = sb("logit", [128, NB, NE])
        topi = sb("topi", [128, NB, 8], U32)
        topf = sb("topf", [128, NB, 2])
        tops = sb("tops", [128, NB, 2])
        iota_e = sb("iota_e", [128, NE])
        comb = sb("comb", [128, NB, NE])
        comb2 = sb("comb2", [128, NB, NE])
        act_g = sb("act_g", [128, 2, 512])
        hid = sb("hid", [128, 2, 512])
        hidT = sb("hidT", [128, 2, 4, J])

        ctxT = shared[:, :].rearrange("p (c b r) -> p c b r", c=HC, b=NB)
        half = shared[:, :].bitcast(BF16)
        NA = (W + 1) * (BR + 1) * 2
        assert 2 * NA <= half.shape[1]
        ups = half[:, 0:NA].rearrange("p (s r t) -> p s r t", s=W + 1, t=2)
        goes = half[:, NA:2 * NA].rearrange("p (s r t) -> p s r t", s=W + 1, t=2)
        spare = ctxn[:, :, :, :].rearrange("p c b h -> p (c b h)")
        zs = spare[:, 0:NB * H].rearrange("p (b h) -> p b h", b=NB)
        hs = spare[:, NB * H:2 * NB * H].rearrange("p (b h) -> p b h", b=NB)

        s_x = sem("x_loaded")
        s_ct = sem("ctx_t_loaded")
        s_cn = sem("ctx_n_loaded")
        s_small = sem("small_loaded")
        s_w = [sem(f"expert_loaded{i}") for i in range(RING)]
        s_pool = sem("constants_ready")
        s_v = sem("vector_step")
        s_var = sem("variances_ready")
        s_std = sem("std_ready")
        s_norm = sem("normed_ready")
        s_tr = sem("transposed")
        s_trc = sem("transposed_copied")
        s_bb = sem("column_norms_ready")
        s_aa = sem("row_norms_ready")
        s_bbp = sem("column_norms_turned")
        s_bbT = sem("column_norms_copied")
        s_dot = sem("products_ready")
        s_sqd = sem("squares_ready")
        s_dist = sem("distances_ready")
        s_skew = [sem(f"distances_skewed{c}") for c in range(NC)]
        s_rows = [sem(f"distance_rows_stored{c}") for c in range(NC)]
        s_prow = [sem(f"path_rows_stored{c}") for c in range(NC)]
        s_back = sem("path_steps")
        s_path = sem("path_copied")
        s_unskew = [sem(f"path_staged{c}") for c in range(NC)]
        s_exp = sem("expanded")
        s_x2 = sem("residual_added")
        s_y = sem("second_norm")
        s_z = sem("third_norm")
        s_att = sem("attn_ready")
        s_h = sem("h_ready")
        s_t = sem("t_ready")
        s_log = sem("logits_ready")
        s_dif = sem("gate_difference")
        s_sig = sem("gate_weights")
        s_gu = sem("gate_up_ready")
        s_silu = sem("silu_ready")
        s_hid = sem("hidden_ready")
        s_ht = sem("hidden_turned")
        s_htc = sem("hidden_copied")
        s_down = sem("down_ready")
        s_acc = sem("expert_added")
        s_out = sem("stored")

        block = stack.enter_context(nc.Block())
        D_BANK = [5, 6, 7, 0, 1, 2]
        ITEMS = [(e, b) for e in range(NE) for b in range(NB)]

        @block.sync
        def _(sp):
            sp.dma_start(xs[0:J, :, :], x).then_inc(s_x, 16)
            sp.dma_start(ctxT[:, :, :, 0:NI], ctx_t).then_inc(s_ct, 16)
            for c in range(NC):
                n = CR if c < NC - 1 else LAST
                sp.dma_start(ctxn[0:n, c, :, :], ctx_n[c * CR:c * CR + n, :, :]).then_inc(s_cn, 16)
            sp.dma_start(attn_w[:, :, :], attn_t).then_inc(s_small, 16)
            sp.dma_start(gate_w[:, :, :], gate_t).then_inc(s_small, 16)
            sp.dma_start(ln_w[:, :, :], ln).then_inc(s_small, 16)
            sp.wait_ge(s_pool, 1)
            for c in range(NC):
                sp.wait_ge(s_dist, 2 * (c + 1))
                sp.dma_start(rows_out[c * CR:(c + 1) * CR, :, :], stage[0:CR, c, :, :]).then_inc(s_rows[c], 16)
            for c in range(NC):
                sp.wait_ge(s_rows[c], 16)
                for k in range(c * CB, (c + 1) * CB):
                    sp.dma_start(big[k:128:KB, :, k:k + J],
                                 rows_out[k * BR:(k + 1) * BR, :, :].rearrange("r b j -> b r j")
                                 ).then_inc(s_skew[c], 16)

            def load_expert(e):
                r = weights[:, e % RING, :]
                n = HC * F
                sp.dma_start(r[:, 0:n], gate_proj[e]).then_inc(s_w[e % RING], 16)
                sp.dma_start(r[:, n:2 * n], up_proj[e]).then_inc(s_w[e % RING], 16)
                sp.dma_start(r[:, 2 * n:3 * n], down_proj[e]).then_inc(s_w[e % RING], 16)

            for e in range(RING):
                load_expert(e)
            sp.wait_ge(s_path, NC)
            for k in range(NC * CB):
                sp.dma_start(rows_back[k * BR:(k + 1) * BR, :, :].rearrange("r b j -> b r j"),
                             big[k:128:KB, :, k:k + J]).then_inc(s_prow[k // CB], 16)
            for c in range(NC):
                sp.wait_ge(s_prow[c], 16 * CB)
                sp.dma_start(stage[0:CR, c, :, :], rows_back[c * CR:(c + 1) * CR, :, :]).then_inc(s_unskew[c], 16)
            for e in range(RING, NE):
                sp.wait_ge(s_down, NB * (e - RING + 1))
                load_expert(e)
            for b in range(NB):
                sp.wait_ge(s_acc, NB * (NE - 1) + b + 1)
                sp.dma_start(out[:, b, :], xs[0:J, b, :]).then_inc(s_out, 16)
            sp.wait_ge(s_out, 16 * NB)

        @block.gpsimd
        def _(pool):
            pool.memset(big[:, :, :], BIG).then_inc(s_pool, 1)
            pool.memset(ident[:, :], 0.0).then_inc(s_pool, 1)
            pool.memset(sel[:, :, :], 1.0).then_inc(s_pool, 1)
            pool.wait_ge(s_pool, 3)
            pool.affine_select(out=ident[:, :], in_=ident[:, :], compare_op=ALU.not_equal, fill=1.0,
                               base=0, pattern=[[-1, 128]], channel_multiplier=1).then_inc(s_pool, 1)
            pool.affine_select(out=sel[:, :, :], in_=sel[:, :, :], compare_op=ALU.is_equal, fill=0.0,
                               base=0, pattern=[[-1, NB], [0, CR]], channel_multiplier=1).then_inc(s_pool, 1)
            pool.memset(ctxT[:, :, :, NI:NC * CR], 0.0).then_inc(s_pool, 1)
            pool.memset(aa[:, :, :], 0.0).then_inc(s_pool, 1)
            pool.memset(eps[:, :], EPS).then_inc(s_pool, 1)
            pool.memset(cost[:, 0, :], BIG).then_inc(s_pool, 1)
            pool.memset(trail[:, :, :], 0.0).then_inc(s_pool, 1)
            pool.iota(iota_e[:, :], pattern=[[1, NE]], base=0, channel_multiplier=0,
                      allow_small_or_imprecise_dtypes=True).then_inc(s_pool, 1)
            pool.wait_ge(s_dot, 6)
            pool.memset(ups[:, :, :, 0], 0.0).then_inc(s_pool, 1)
            pool.memset(ups[:, :, :, 1], 1.0).then_inc(s_pool, 1)
            pool.memset(goes[:, :, :, :], 0.0).then_inc(s_pool, 1)

        POOL_EARLY = 11
        POOL_ALL = POOL_EARLY + 3

        @block.scalar
        def _(act):
            act.wait_ge(s_cn, 16 * NC)
            act.wait_ge(s_pool, POOL_EARLY)
            for c in range(NC):
                n = CR if c < NC - 1 else LAST
                for b in range(NB):
                    if c + b:
                        act.wait_ge(s_aa, c * NB + b)
                    nc.scalar.activation(sq[0:n, :], ctxn[0:n, c, b, :], ACT.Square,
                                         accum_out=aa[0:n, c, b:b + 1]).then_inc(s_aa, 1)
            act.wait_ge(s_var, 1)
            nc.scalar.activation(std[0:J, :], mv[0:J, :, 1], ACT.Sqrt, bias=eps[0:J, :]).then_inc(s_std, 1)
            for b in range(NB):
                act.wait_ge(s_norm, b + 1)
                act.wait_ge(s_aa, NC * NB + b)
                nc.scalar.activation(sq[0:J, :], xn[0:J, b, :], ACT.Square,
                                     accum_out=bb[0:J, b:b + 1]).then_inc(s_aa, 1)
            for c in range(HC):
                for h in range(2):
                    act.wait_ge(s_tr, 2 * c + h + 1)
                    nc.scalar.activation(xT[:, c, G * h:G * h + G, :],
                                         bank[2 * c + h][:, 0:G * J].rearrange("p (b j) -> p b j", b=G),
                                         ACT.Copy, scale=-2.0).then_inc(s_trc, 1)
            for n in range(2 * NC):
                act.wait_ge(s_sqd, G * (n + 1))
                c, h = n // 2, n % 2
                v = stage[0:CR, c, G * h:G * h + G, :]
                nc.scalar.activation(v, v, ACT.Sqrt).then_inc(s_dist, 1)
            for n in range(NC):
                s0, s1 = W * (NC - 1 - n) // NC, W * (NC - n) // NC
                act.wait_ge(s_back, W - s0)
                nc.scalar.activation(big[:, :, s0:s1].rearrange("p r w -> p w r"),
                                     trail[:, s0:s1, 2:2 * BR + 1:2][:, :, ::-1],
                                     ACT.Copy).then_inc(s_path, 1)
            for n in range(3):
                for g in range(2):
                    act.wait_ge(s_var, 2 + 2 * n + g)
                    nc.scalar.activation(std[0:J, G * g:G * g + G], mv[0:J, G * g:G * g + G, 1],
                                         ACT.Sqrt, bias=eps[0:J, :]).then_inc(s_std, 1)
                if n == 1:
                    act.wait_ge(s_small, 48)
                if n >= 1:
                    for b in range(NB):
                        act.wait_ge(s_tr, 4 + (n - 1) * NB + b + 1)
                        if n == 2:
                            act.wait_ge(s_att, NB)
                        for c in range(HC):
                            last = nc.scalar.activation(xT[:, c, b, :], bank[2 + b % 2][:, c * J:(c + 1) * J],
                                                        ACT.Identity, scale=ln_w[:, 2 * n - 2, c:c + 1],
                                                        bias=ln_w[:, 2 * n - 1, c:c + 1])
                        last.then_inc(s_trc, 1)
            act.wait_ge(s_dif, 1)
            nc.scalar.activation(tops[0:J, :, :], tops[0:J, :, :], ACT.Sigmoid).then_inc(s_sig, 1)
            for n in range(2 * len(ITEMS)):
                q = n % 2
                act.wait_ge(s_gu, n + 1)
                if n >= 2:
                    act.wait_ge(s_hid, n - 1)
                nc.scalar.activation(act_g[0:J, q, :], bank[q][0:J, :], ACT.Silu).then_inc(s_silu, 1)
                if n >= 1:
                    m = n - 1
                    act.wait_ge(s_ht, m + 1)
                    if m >= 2:
                        act.wait_ge(s_down, (m - 2) // 2 + 1)
                    nc.scalar.activation(hidT[:, m % 2, :, :], bank[4 + m % 2][:, 0:4 * J].rearrange("p (f j) -> p f j", f=4),
                                         ACT.Copy).then_inc(s_htc, 1)
            m = 2 * len(ITEMS) - 1
            act.wait_ge(s_ht, m + 1)
            act.wait_ge(s_down, (m - 2) // 2 + 1)
            nc.scalar.activation(hidT[:, m % 2, :, :], bank[4 + m % 2][:, 0:4 * J].rearrange("p (f j) -> p f j", f=4),
                                 ACT.Copy).then_inc(s_htc, 1)

        @block.vector
        def _(dve):
            done = [0]

            def link(ins):
                done[0] += 1
                ins.then_inc(s_v, 1)
                dve.wait_ge(s_v, done[0])

            def stats(g0, g1):
                for b in range(g0, g1):
                    last = nc.vector.bn_stats(out=bn6[0:J, b, :], in_=xs_of[b])
                link(last)
                for b in range(g0, g1):
                    last = nc.vector.bn_aggr(out=mv[0:J, b, :], in_=bn6[0:J, b, :])
                last.then_inc(s_var, 1)

            dve.wait_ge(s_x, 16)
            xs_of = [xs[0:J, b, :] for b in range(NB)]
            stats(0, NB)
            dve.wait_ge(s_std, 1)
            dve.wait_ge(s_var, 1)
            link(nc.vector.reciprocal(rstd[0:J, :], std[0:J, :]))
            for b in range(NB):
                nc.vector.tensor_scalar(xn[0:J, b, :], xs[0:J, b, :], mv[0:J, b, 0:1], rstd[0:J, b:b + 1],
                                        ALU.subtract, ALU.mult).then_inc(s_norm, 1)
            dve.wait_ge(s_bbp, 1)
            nc.vector.tensor_copy(bbT[:, :], bank[4][0:NB, 0:J]).then_inc(s_bbT, 1)
            dve.wait_ge(s_aa, NC * NB)
            for n in range(2 * NC):
                dve.wait_ge(s_dot, n + 1)
                c, h = n // 2, n % 2
                for b in range(G * h, G * h + G):
                    nc.vector.tensor_scalar(stage[0:CR, c, b, :], bank[D_BANK[n]][0:CR, (b % G) * J:(b % G + 1) * J],
                                            aa[0:CR, c, b:b + 1], 0.0, ALU.add, ALU.max).then_inc(s_sqd, 1)
            dve.wait_ge(s_pool, POOL_EARLY)
            nc.vector.memset(seed[:, :], 0.0)
            nc.vector.tensor_reduce(first[:, 0:1], ident[:, 0:128:KB], AX_X, ALU.add)
            link(nc.vector.tensor_reduce(first[:, 1:2], ident[:, END_K:128:KB], AX_X, ALU.add))
            nc.vector.tensor_scalar(cost[:, 0, 0:1], first[:, 0:1], -BIG, BIG, ALU.mult, ALU.add)
            at = 2 * (BR - 1 - END_R) + 1
            link(nc.vector.tensor_copy(seed[:, at:at + 1], first[:, 1:2]))
            for s in range(W):
                if s % CB == 0 and s // CB < NC:
                    dve.wait_ge(s_skew[s // CB], 16 * CB)
                nc.vector.stream_shuffle(cost[:, s + 1, 0:1], cost[:, s, BR:BR + 1],
                                         [(p & 16) | ((p - 1) & 15) for p in range(32)]).then_inc(s_v, 1)
                nc.vector.tensor_tensor(best[:, s % 2, :], cost[:, s, 0:BR], cost[:, s, 1:BR + 1], ALU.min).then_inc(s_v, 1)
                done[0] += 2
                dve.wait_ge(s_v, done[0])
                link(nc.vector.tensor_tensor_scan(cost[:, s + 1, 1:BR + 1], best[:, s % 2, :], big[:, :, s],
                                                  cost[:, s + 1, 0:1], ALU.min, ALU.add))
            dve.wait_ge(s_pool, POOL_ALL)
            up_c, dg_c, lf_c = cost[:, 1:W + 1, 0:BR], cost[:, 0:W, 0:BR], cost[:, 0:W, 1:BR + 1]
            up_o = ups[:, 0:W, BR:0:-1, 0]
            dg_o = goes[:, 0:W, BR:0:-1, 0]
            lf_o = goes[:, 0:W, BR - 1::-1, 1]
            least = big[:, :, :].rearrange("p r w -> p (r w)").rearrange("p (w r) -> p w r", r=BR)
            link(nc.vector.tensor_tensor(least, up_c, lf_c, ALU.min))
            nc.vector.tensor_tensor(up_o, up_c, lf_c, ALU.is_le)
            link(nc.vector.tensor_tensor(dg_o, dg_c, least, ALU.is_le))
            link(nc.vector.tensor_tensor(up_o, dg_o, up_o, ALU.is_lt))
            link(nc.vector.tensor_tensor(lf_o, dg_o, up_o, ALU.is_equal))
            down = [(p & 16) | min((p & 15) + 1, 15) for p in range(32)]
            for m in (ups, goes):
                link(nc.vector.stream_shuffle(m[:, 0:W - 1, 0, 0], m[:, 1:W, BR, 0], down))
            step0 = step_in[:, 0, :]
            link(nc.vector.tensor_copy(step0, seed[:, :]))
            for s in reversed(range(W)):
                if s < W - 1:
                    nc.vector.stream_shuffle(trail[:, s, 0:1], trail[:, s + 1, 2 * BR:2 * BR + 1], down).then_inc(s_v, 1)
                    t = trail[:, s + 1, 0:2]
                    pair = bass.AP(tensor=t.tensor, offset=t.offset, ap=[list(t.ap[0]), [2, BR], [2, 2]])
                    nc.vector.tensor_tensor(step0.rearrange("p (r t) -> p r t", t=2), pair,
                                            goes[:, s + 1, 0:BR, :], ALU.mult).then_inc(s_v, 1)
                    done[0] += 2
                    dve.wait_ge(s_v, done[0])
                nc.vector.tensor_tensor_scan(trail[:, s, 1:2 * BR + 1],
                                             ups[:, s, 0:BR, :].rearrange("p r t -> p (r t)"), step0,
                                             trail[:, s, 0:1], ALU.mult, ALU.add).then_inc(s_back, 1)
                dve.wait_ge(s_back, W - s)

            for b in range(NB):
                dve.wait_ge(s_exp, b + 1)
                nc.vector.tensor_tensor(xs[0:J, b, :], xs[0:J, b, :], bank[b % 2][0:J, 0:H], ALU.add).then_inc(s_x2, 1)
            srcs = [xs, xn, xn]
            for n in range(3):
                if n == 2:
                    for b in range(NB):
                        dve.wait_ge(s_att, b + 1)
                        dve.wait_ge(s_y, b + 1)
                        nc.vector.tensor_tensor(hs[0:J, b, :], xn[0:J, b, :], bank[4 + b % 2][0:J, 0:H],
                                                ALU.add).then_inc(s_h, 1)
                src = [xs, xn, hs][n]
                dst = [xn, zs, zs][n]
                up = [s_y, s_z, s_t][n]
                got = [s_x2, s_y, s_h][n]
                xs_of = [src[0:J, b, :] for b in range(NB)]
                dve.wait_ge(got, NB)
                if n:
                    dve.wait_ge([None, s_y, s_z][n], NB)
                for g in range(2):
                    stats(G * g, G * g + G)
                    dve.wait_ge(s_std, 2 + 2 * n + g)
                    dve.wait_ge(s_var, 2 + 2 * n + g)
                    link(nc.vector.reciprocal(rstd[0:J, G * g:G * g + G], std[0:J, G * g:G * g + G]))
                    for b in range(G * g, G * g + G):
                        if n == 2:
                            dve.wait_ge(s_tr, 4 + b + 1)
                        nc.vector.tensor_scalar(dst[0:J, b, :], src[0:J, b, :], mv[0:J, b, 0:1], rstd[0:J, b:b + 1],
                                                ALU.subtract, ALU.mult).then_inc(up, 1)
            for b in range(NB):
                last = nc.vector.tensor_tensor(xs[0:J, b, :], xs[0:J, b, :], hs[0:J, b, :], ALU.add)
            link(last)
            dve.wait_ge(s_log, NB)
            link(nc.vector.tensor_copy(logit[0:J, :, :], bank[6][0:J, 0:NB * NE].rearrange("p (b e) -> p b e", b=NB)))
            for b in range(NB):
                last = nc.vector.max(out=top[0:J, b, :], in_=logit[0:J, b, :])
            link(last)
            for b in range(NB):
                nc.vector.max_index(out=topi[0:J, b, :], in_max=top[0:J, b, :], in_values=logit[0:J, b, :])
            nc.vector.tensor_tensor(tops[0:J, :, 0], top[0:J, :, 0], top[0:J, :, 1], ALU.subtract)
            link(nc.vector.tensor_tensor(tops[0:J, :, 1], top[0:J, :, 1], top[0:J, :, 0], ALU.subtract))
            link(nc.vector.tensor_copy(topf[0:J, :, :], topi[0:J, :, 0:2]))
            dve.sem_inc(s_dif, 1)
            dve.wait_ge(s_sig, 1)
            for b in range(NB):
                nc.vector.tensor_scalar(comb[0:J, b, :], iota_e[0:J, :], topf[0:J, b, 0:1], tops[0:J, b, 0:1],
                                        ALU.is_equal, ALU.mult)
                last = nc.vector.tensor_scalar(comb2[0:J, b, :], iota_e[0:J, :], topf[0:J, b, 1:2], tops[0:J, b, 1:2],
                                               ALU.is_equal, ALU.mult)
            link(last)
            link(nc.vector.tensor_tensor(comb[0:J, :, :], comb[0:J, :, :], comb2[0:J, :, :], ALU.add))
            for n in range(2 * len(ITEMS)):
                q = n % 2
                dve.wait_ge(s_silu, n + 1)
                if n >= 2:
                    dve.wait_ge(s_ht, n - 1)
                nc.vector.tensor_tensor(hid[0:J, q, :], act_g[0:J, q, :], bank[2 + q][0:J, :], ALU.mult).then_inc(s_hid, 1)
                if q == 1 and n >= 3 or n == 2 * len(ITEMS) - 1:
                    for m in ([n // 2 - 1] if n < 2 * len(ITEMS) - 1 else [n // 2 - 1, n // 2]):
                        e, b = ITEMS[m]
                        dve.wait_ge(s_down, m + 1)
                        if e:
                            dve.wait_ge(s_acc, NB * (e - 1) + b + 1)
                        nc.vector.scalar_tensor_tensor(xs[0:J, b, :], bank[6 + m % 2][0:J, 0:H], comb[0:J, b, e:e + 1],
                                                       xs[0:J, b, :], ALU.mult, ALU.add).then_inc(s_acc, 1)

        @block.tensor
        def _(pe):
            pe.wait_ge(s_pool, POOL_EARLY)
            for c in range(HC):
                for h in range(2):
                    for b in range(G * h, G * h + G):
                        pe.wait_ge(s_norm, b + 1)
                        last = nc.tensor.transpose(bank[2 * c + h][:, (b % G) * J:(b % G + 1) * J],
                                                   xn[0:J, b, c * 128:(c + 1) * 128], ident[0:J, 0:J])
                    last.then_inc(s_tr, 1)
            pe.wait_ge(s_aa, NC * NB + NB)
            nc.tensor.transpose(bank[4][0:NB, 0:J], bb[0:J, :], ident[0:J, 0:J]).then_inc(s_bbp, 1)
            pe.wait_ge(s_bbT, 1)
            pe.wait_ge(s_ct, 16)
            pe.wait_ge(s_trc, 4)
            for n in range(2 * NC):
                c, h = n // 2, n % 2
                for b in range(G * h, G * h + G):
                    o = bank[D_BANK[n]][0:CR, (b % G) * J:(b % G + 1) * J]
                    for kc in range(HC):
                        nc.tensor.matmul(o, ctxT[:, kc, b, c * CR:(c + 1) * CR], xT[:, kc, b, :],
                                         start=(kc == 0), stop=False)
                    last = nc.tensor.matmul(o, sel[:, b, :], bbT[:, :], start=False, stop=True)
                last.then_inc(s_dot, 1)
            for c in range(NC):
                pe.wait_ge(s_unskew[c], 16)
            for b in range(NB):
                if b >= 2:
                    pe.wait_ge(s_x2, b - 1)
                for c in range(NC):
                    n = CR if c < NC - 1 else LAST
                    last = nc.tensor.matmul(bank[b % 2][0:J, 0:H], stage[0:n, c, b, :], ctxn[0:n, c, b, :],
                                            start=(c == 0), stop=(c == NC - 1))
                last.then_inc(s_exp, 1)

            def turn(n, src_sem):
                for b in range(NB):
                    pe.wait_ge(src_sem, b + 1)
                    if b >= 2:
                        pe.wait_ge(s_trc, 4 + n * NB + b - 1)
                    for c in range(HC):
                        last = nc.tensor.transpose(bank[2 + b % 2][:, c * J:(c + 1) * J],
                                                   zs[0:J, b, c * 128:(c + 1) * 128], ident[0:J, 0:J])
                    last.then_inc(s_tr, 1)

            turn(0, s_z)
            pe.wait_ge(s_small, 48)
            for b in range(NB):
                pe.wait_ge(s_trc, 4 + b + 1)
                if b >= 2:
                    pe.wait_ge(s_h, b - 1)
                for c in range(HC):
                    last = nc.tensor.matmul(bank[4 + b % 2][0:J, 0:H], xT[:, c, b, :], attn_w[:, c, :],
                                            start=(c == 0), stop=(c == HC - 1))
                last.then_inc(s_att, 1)
            turn(1, s_t)
            for b in range(NB):
                pe.wait_ge(s_trc, 4 + NB + b + 1)
                for c in range(HC):
                    last = nc.tensor.matmul(bank[6][0:J, b * NE:(b + 1) * NE], xT[:, c, b, :], gate_w[:, c, :],
                                            start=(c == 0), stop=(c == HC - 1))
                last.then_inc(s_log, 1)

            def gate_up(n):
                q = n % 2
                e, b = ITEMS[n // 2]
                if b == 0 and q == 0:
                    pe.wait_ge(s_w[e % RING], 48 * (e // RING + 1))
                if n >= 2:
                    pe.wait_ge(s_hid, n - 1)
                for k in range(2):
                    for c in range(HC):
                        o = k * HC * F + c * F + q * 512
                        last = nc.tensor.matmul(bank[2 * k + q][0:J, :], xT[:, c, b, :],
                                                weights[:, e % RING, o:o + 512],
                                                start=(c == 0), stop=(c == HC - 1))
                last.then_inc(s_gu, 1)

            def turn_down(n):
                q = n % 2
                m = n // 2
                e, b = ITEMS[m]
                pe.wait_ge(s_hid, n + 1)
                if n >= 2:
                    pe.wait_ge(s_htc, n - 1)
                for f in range(4):
                    last = nc.tensor.transpose(bank[4 + q][:, f * J:(f + 1) * J], hid[0:J, q, f * 128:(f + 1) * 128],
                                               ident[0:J, 0:J])
                last.then_inc(s_ht, 1)
                pe.wait_ge(s_htc, n + 1)
                if q == 0:
                    if m >= 2:
                        pe.wait_ge(s_acc, m - 1)
                    if m == 0:
                        pe.wait_ge(s_dif, 1)
                for f in range(4):
                    o = 2 * HC * F + (4 * q + f) * H
                    last = nc.tensor.matmul(bank[6 + m % 2][0:J, 0:H], hidT[:, q, f, :],
                                            weights[:, e % RING, o:o + H],
                                            start=(q == 0 and f == 0), stop=(q == 1 and f == 3))
                if q == 1:
                    last.then_inc(s_down, 1)

            gate_up(0)
            for n in range(1, 2 * len(ITEMS)):
                gate_up(n)
                turn_down(n - 1)
            turn_down(2 * len(ITEMS) - 1)


def kernel(x, ctx_1024, L0_ffn_ln1_g, L0_ffn_ln1_b, L0_ffn_attn_w, L0_ffn_ln2_g, L0_ffn_ln2_b,
           L0_ffn_gate_w, L0_ffn_gate_proj, L0_ffn_up_proj, L0_ffn_down_proj):
    import numpy as np
    import concourse.bacc as bacc
    from concourse.bass_utils import run_bass_kernel_spmd

    def by_partition(a, axis):
        a = np.moveaxis(np.asarray(a), axis, 0)
        return np.moveaxis(a.reshape((a.shape[0] // 128, 128) + a.shape[1:]), 0, 1)

    ctx = np.asarray(ctx_1024)
    ln = np.stack([np.asarray(v) for v in (L0_ffn_ln1_g, L0_ffn_ln1_b, L0_ffn_ln2_g, L0_ffn_ln2_b)])
    laid = {
        "x": np.asarray(x).transpose(1, 0, 2),
        "ctx_t": by_partition(ctx, 2),
        "ctx_n": ctx.transpose(1, 0, 2),
        "ln": by_partition(ln, 1).transpose(0, 2, 1),
        "attn_t": by_partition(L0_ffn_attn_w, 1),
        "gate_t": by_partition(L0_ffn_gate_w, 1),
        "gate_proj": np.stack([by_partition(w, 1) for w in np.asarray(L0_ffn_gate_proj)]).reshape(NE, 128, HC * F),
        "up_proj": np.stack([by_partition(w, 1) for w in np.asarray(L0_ffn_up_proj)]).reshape(NE, 128, HC * F),
        "down_proj": np.stack([by_partition(w, 1) for w in np.asarray(L0_ffn_down_proj)]).reshape(NE, 128, FC * H),
    }
    nc = bacc.Bacc("TRN2", target_bir_lowering=False, num_devices=1)
    arrays, args = {}, []
    for name, a in laid.items():
        arrays[name] = np.ascontiguousarray(a)
        args.append(nc.dram_tensor(name, a.shape, mybir.dt.from_np(a.dtype), kind="ExternalInput").ap())
    args.append(nc.dram_tensor("out", (J, NB, H), F32, kind="ExternalOutput").ap())
    align_and_route(nc, *args)
    got = run_bass_kernel_spmd(nc, [arrays], core_ids=[0]).results[0]["out"]
    return np.ascontiguousarray(got.transpose(1, 0, 2))
```

```python
from contextlib import ExitStack

import concourse.bass as bass
from concourse import mybir

F32 = mybir.dt.float32
BF16 = mybir.dt.bfloat16
U32 = mybir.dt.uint32
I32 = mybir.dt.int32
ALU = mybir.AluOpType
ACT = mybir.ActivationFunctionType
AX_X = mybir.AxisListType.X

NB = 8
J = 100
NI = 361
H = 256
HC = H // 128
F = 1024
FC = F // 128
NE = 8
BR = 25
KB = 16
NK = -(-NI // BR)
CB = 4
CR = CB * BR
NC = -(-NI // CR)
ROWS = [min(CR, NI - c * CR) for c in range(NC)]
BLOCKS = [min(CB, NK - c * CB) for c in range(NC)]
W = J + NK - 1
END_K, END_R = (NI - 1) // BR, (NI - 1) % BR
G = 4
BIG = 1e30
EPS = 1e-5
RING = 3
TOP = 2
ST = 128
NT = (TOP * NB * J + NE * (ST - 1)) // ST
MT = -(-NB * J // ST)
ROW = H + 4
ID, W2, WD, E1 = H, H + 1, H + 2, H + 3
EW = 3 * HC * F


def align_and_route(nc, x, ctx_t, ctx_n, ln, attn_t, gate_t, gate_proj, up_proj, down_proj, out):
    with ExitStack() as stack:
        def sb(name, shape, dt=F32):
            return stack.enter_context(nc.sbuf_tensor(name, shape, dt))

        def sem(name):
            return stack.enter_context(nc.semaphore(name))

        bank = [stack.enter_context(nc.psum_tensor(f"bank{i}", [128, 512], F32)) for i in range(8)]

        rows_out = nc.dram_tensor("distance_rows", (NK * BR, NB, J), F32, kind="Internal").ap()
        rows_back = nc.dram_tensor("path_rows", (NK * BR, NB, J), F32, kind="Internal").ap()

        routed = nc.dram_tensor("routed_rows", (NT * ST, ROW), F32, kind="Internal").ap()

        weights = sb("weights", [128, RING, EW])
        big = sb("big", [128, BR, W])
        cost = sb("cost", [128, W + 1, BR + 1])
        shared = sb("shared", [128, W * (BR + 1) * 2])
        trail = sb("trail", [128, W, 2 * BR + 1], BF16)
        stage = sb("stage", [128, NC, NB, J])
        ctxn = sb("ctxn", [128, NC, NB, H])
        xs = sb("xs", [128, NB, H])
        xn = sb("xn", [128, NB, H])
        xT = sb("xT", [128, HC, NB, J])
        attn_w = sb("attn_w", [128, HC, H])
        gate_w = sb("gate_w", [128, HC, NE])
        ln_w = sb("ln_w", [128, 4, HC])
        ident = sb("ident", [128, 128])
        quarter = sb("quarter", [128, CR])
        seed = sb("seed", [128, 2 * BR], BF16)
        first = sb("first", [128, 2])
        bn6 = sb("bn6", [128, NB, 6])
        mv = sb("mv", [128, NB, 2])
        std = sb("std", [128, NB])
        rstd = sb("rstd", [128, NB])
        aa = sb("aa", [128, NC, NB])
        eps = sb("eps", [128, 1])
        best = sb("best", [128, 2, BR])
        step_in = sb("step_in", [128, 2, 2 * BR], BF16)
        top = sb("top", [128, NB, 8])
        logit = sb("logit", [128, NB, NE])
        topi = sb("topi", [128, NB, 8], U32)
        topf = sb("topf", [128, NB, 2])
        tops = sb("tops", [128, NB, 2])
        iota_e = sb("iota_e", [128, NE])
        picked = sb("picked", [128, TOP, NB, NE])
        chosen = sb("chosen", [128, NB, NE], BF16)
        before = sb("before", [128, ST], BF16)
        ones = sb("ones", [128, 128], BF16)
        count = sb("count", [128, NE])
        steps = sb("steps", [128, MT])
        more = sb("more", [128, NE, MT])
        tiles = sb("tiles", [128, NE])
        zero8 = sb("zero8", [128, NE])
        ends = sb("ends", [128, NE])
        base = sb("base", [128, NE])
        place = sb("place", [128, NB, NE])
        hit = sb("hit", [128, TOP, NB, NE])
        placef = sb("placef", [128, TOP, NB])
        slot = sb("slot", [128, TOP, NB], U32)
        tile_no = sb("tile_no", [128, NT])
        passed = sb("passed", [128, NT, NE])
        tile_e = sb("tile_e", [128, NT])
        wrap = sb("wrap", [128, 2, NT])
        tile_w = sb("tile_w", [128, NT])
        table = sb("table", [1, 2, NT], I32)
        ends_i = sb("ends_i", [1, NE], I32)
        blank = sb("blank", [128, ROW])
        slot_w = sb("slot_w", [128, NT])
        flat = cost[:, :, :].rearrange("p s r -> p (s r)")
        act_g = flat[:, 0:1024].rearrange("p (q f) -> p q f", q=2)
        hid = flat[:, 1024:2048].rearrange("p (q f) -> p q f", q=2)
        row_in = flat[:, 2048:2560].rearrange("p (q h) -> p q h", q=2)
        flat = big[:, :, :].rearrange("p r w -> p (r w)")
        hidT = flat[:, 0:1024].rearrange("p (q f s) -> p q f s", q=2, f=4)
        tT = flat[:, 1024:1536].rearrange("p (q c s) -> p q c s", q=2, c=HC)
        scaled = flat[:, 1536:2048].rearrange("p (q h) -> p q h", q=2)
        token = sb("token", [128, 2], U32)

        ctxT = [shared[:, HC * NB * c * CR:HC * NB * (c * CR + ROWS[c])].rearrange("p (k b r) -> p k b r", k=HC, b=NB)
                for c in range(NC)]
        sq = cost[:, :, :].rearrange("p s r -> p (s r)")[:, 2048:2048 + H]
        xsq = cost[:, :, :].rearrange("p s r -> p (s r)")[:, BR + 1:BR + 1 + HC * NB * J].rearrange(
            "p (c b j) -> p c b j", c=HC, b=NB)
        bb = xn[0:CR, :, :].rearrange("p b h -> p (b h)")[:, 0:NB * J].rearrange("p (h n) -> p h n", h=2)
        half = shared[:, :].bitcast(BF16)
        NA = W * (BR + 1) * 2
        ups = half[:, 0:NA].rearrange("p (s r t) -> p s r t", s=W, t=2)
        goes = half[:, NA:2 * NA].rearrange("p (s r t) -> p s r t", s=W, t=2)
        spare = ctxn[:, :, :, :].rearrange("p c b h -> p (c b h)")
        zs = spare[:, 0:NB * ROW].rearrange("p (b h) -> p b h", b=NB)
        hs = spare[:, NB * ROW:NB * (ROW + H)].rearrange("p (b h) -> p b h", b=NB)
        rows = shared[:, 0:NT * ROW].rearrange("p (t h) -> p t h", t=NT)
        wflat = weights[:, :, :].rearrange("p r n -> p (r n)")

        s_x = sem("x_loaded")
        s_ct = [sem(f"ctx_t_loaded{c}") for c in range(NC)]
        s_cn = [sem(f"ctx_n_loaded{c}") for c in range(NC)]
        s_small = sem("small_loaded")
        s_w = [sem(f"expert_loaded{i}") for i in range(RING)]
        s_pool = sem("constants_ready")
        s_v = sem("vector_step")
        s_var = sem("variances_ready")
        s_std = sem("std_ready")
        s_norm = sem("normed_ready")
        s_tr = sem("transposed")
        s_trc = sem("transposed_copied")
        s_xsq = sem("squares_of_x")
        s_bb = sem("column_norms_ready")
        s_aa = sem("row_norms_ready")
        s_dot = sem("products_ready")
        s_sqd = sem("squares_ready")
        s_dist = sem("distances_ready")
        s_skew = [sem(f"distances_skewed{c}") for c in range(NC)]
        s_rows = [sem(f"distance_rows_stored{c}") for c in range(NC)]
        s_prow = [sem(f"path_rows_stored{c}") for c in range(NC)]
        s_back = sem("path_steps")
        s_path = sem("path_copied")
        s_unskew = [sem(f"path_staged{c}") for c in range(NC)]
        s_exp = sem("expanded")
        s_x2 = sem("residual_added")
        s_y = sem("second_norm")
        s_z = sem("third_norm")
        s_att = sem("attn_ready")
        s_h = sem("h_ready")
        s_t = sem("t_ready")
        s_log = sem("logits_ready")
        s_sum = sem("x_plus_h_ready")
        s_dif = sem("gate_difference")
        s_sig = sem("gate_weights")
        s_gu = sem("gate_up_ready")
        s_silu = sem("silu_ready")
        s_hid = sem("hidden_ready")
        s_ht = sem("hidden_turned")
        s_htc = sem("hidden_copied")
        s_down = sem("down_ready")
        s_o = sem("tile_scaled")
        s_rin = sem("tile_rows_copied")
        s_in = sem("tile_inputs_ready")
        s_in_t = sem("tile_inputs_turned")
        s_ready = sem("experts_ready")
        s_blank = sem("routed_rows_cleared")
        s_rank = sem("ranks_ready")
        s_pick = sem("choices_for_ranks")
        s_slot = sem("slots_ready")
        s_table = sem("tables_ready")
        s_scat = sem("rows_routed")
        s_load = [sem(f"routed_rows_loaded{i}") for i in range(NT // 4)]
        s_tiles = sem("tiles_on_chip")
        s_init = sem("output_started")
        s_added = sem("tile_added")

        block = stack.enter_context(nc.Block())
        POOL_FIRST = 4
        POOL_EARLY = 7
        POOL_ALL = POOL_EARLY + 12
        COPIES = [(76, W), (44, 76), (12, 44), (8, 12), (4, 8), (0, 4)]
        D_BANK = [4, 5, 6, 7, 2, 3]

        @block.sync
        def _(sp):
            sp.dma_start(xs[0:J, :, :], x).then_inc(s_x, 16)
            for c in range(NC):
                n, o = ROWS[c], HC * NB * c * CR
                sp.dma_start(shared[:, o:o + HC * NB * n], ctx_t[:, o:o + HC * NB * n]).then_inc(s_ct[c], 16)
                sp.dma_start(ctxn[0:n, c, :, :], ctx_n[c * CR:c * CR + n, :, :]).then_inc(s_cn[c], 16)
            sp.dma_start(attn_w[:, :, :], attn_t).then_inc(s_small, 16)
            sp.dma_start(gate_w[:, :, :], gate_t).then_inc(s_small, 16)
            sp.dma_start(ln_w[:, :, :], ln).then_inc(s_small, 16)
            sp.wait_ge(s_pool, POOL_EARLY)
            for c in range(NC):
                sp.wait_ge(s_rows[c], 16)
                for k in range(c * CB, c * CB + BLOCKS[c]):
                    sp.dma_start(big[k:128:KB, :, k:k + J],
                                 rows_out[k * BR:(k + 1) * BR, :, :].rearrange("r b j -> b r j")
                                 ).then_inc(s_skew[c], 16)

            def load_expert(e):
                r = weights[:, e % RING, :]
                n = HC * F
                sp.dma_start(r[:, 0:n], gate_proj[e]).then_inc(s_w[e % RING], 16)
                sp.dma_start(r[:, n:2 * n], up_proj[e]).then_inc(s_w[e % RING], 16)
                sp.dma_start(r[:, 2 * n:3 * n], down_proj[e]).then_inc(s_w[e % RING], 16)

            for e in range(RING):
                load_expert(e)
            for n, c in enumerate(reversed(range(NC))):
                sp.wait_ge(s_path, len(COPIES) - NC + 1 + n)
                for k in range(c * CB, c * CB + BLOCKS[c]):
                    sp.dma_start(rows_back[k * BR:(k + 1) * BR, :, :].rearrange("r b j -> b r j"),
                                 big[k:128:KB, :, k:k + J]).then_inc(s_prow[c], 16)
            for e in range(RING):
                sp.wait_ge(s_w[e], 48)
                sp.sem_inc(s_ready, 1)
            sp.wait_ge(s_sum, 1)
            sp.dma_start(out[0:NB * J, :].rearrange("(b j) h -> j b h", b=NB), xs[0:J, :, :]).then_inc(s_init, 16)
            sp.wait_ge(s_scat, 16 * TOP * NB)
            for i in range(NT // 4):
                sp.dma_start(rows[:, 4 * i:4 * i + 4, :],
                             routed[4 * i * ST:4 * (i + 1) * ST, :].rearrange("(t p) h -> p t h", p=ST)
                             ).then_inc(s_load[i], 16)
            for i in range(NT // 4):
                sp.wait_ge(s_load[i], 16)
                sp.sem_inc(s_tiles, 4)
            sp.wait_ge(s_table, 1)
            for e in range(RING, NE):
                last_tile = sp.value_load(ends_i[0:1, e - RING:e - RING + 1], min_val=0, max_val=NT)
                sp.wait_ge(s_down, last_tile * 2 + 1)
                load_expert(e)
                sp.wait_ge(s_w[e % RING], 48 * (e // RING + 1))
                sp.sem_inc(s_ready, 1)

        @block.gpsimd
        def _(pool):
            pool.memset(ident[:, :], 0.0).then_inc(s_pool, 1)
            pool.memset(eps[:, :], EPS).then_inc(s_pool, 1)
            pool.wait_ge(s_pool, 2)
            pool.affine_select(out=ident[:, :], in_=ident[:, :], compare_op=ALU.not_equal, fill=1.0,
                               base=0, pattern=[[-1, 128]], channel_multiplier=1).then_inc(s_pool, 1)
            pool.memset(quarter[:, :], 0.25).then_inc(s_pool, 1)
            pool.memset(stage[:, NC - 1, :, :], 0.0).then_inc(s_pool, 1)
            pool.memset(big[:, :, :], BIG).then_inc(s_pool, 1)
            pool.memset(cost[:, 0, :], BIG).then_inc(s_pool, 1)
            pool.iota(iota_e[:, :], pattern=[[1, NE]], base=0, channel_multiplier=0,
                      allow_small_or_imprecise_dtypes=True).then_inc(s_pool, 1)
            pool.iota(steps[:, :], pattern=[[ST, MT]], base=0, channel_multiplier=0,
                      allow_small_or_imprecise_dtypes=True).then_inc(s_pool, 1)
            pool.iota(tile_no[:, :], pattern=[[1, NT]], base=0, channel_multiplier=0,
                      allow_small_or_imprecise_dtypes=True).then_inc(s_pool, 1)
            pool.memset(zero8[:, :], 0.0).then_inc(s_pool, 1)
            pool.memset(ones[:, :], 1.0).then_inc(s_pool, 1)
            pool.memset(before[:, :], 1.0).then_inc(s_pool, 1)
            pool.memset(blank[:, :], 0.0).then_inc(s_pool, 1)
            pool.wait_ge(s_pool, POOL_EARLY + 7)
            pool.affine_select(out=before[:, :], in_=before[:, :], compare_op=ALU.is_gt, fill=0.0,
                               base=0, pattern=[[1, ST]], channel_multiplier=-1).then_inc(s_pool, 1)
            pool.iota(blank[:, ID:ID + 1], pattern=[[0, 1]], base=NB * J, channel_multiplier=1,
                      allow_small_or_imprecise_dtypes=True).then_inc(s_pool, 1)
            pool.wait_ge(s_pool, POOL_EARLY + 9)
            for t in range(NT):
                pool.dma_start(routed[t * ST:(t + 1) * ST, :], blank[:, :]).then_inc(s_blank, 16)
            pool.wait_ge(s_dot, 2 * NC)
            pool.memset(ups[:, :, :, 1], 1.0).then_inc(s_pool, 1)
            pool.memset(ups[:, W - 1, 0, 0:1], 0.0).then_inc(s_pool, 1)
            pool.memset(goes[:, W - 1, 0, 0:1], 0.0).then_inc(s_pool, 1)
            pool.wait_ge(s_exp, NB)
            pool.iota(zs[:, :, ID], pattern=[[J, NB]], base=0, channel_multiplier=1,
                      allow_small_or_imprecise_dtypes=True).then_inc(s_pool, 1)
            pool.wait_ge(s_pool, POOL_ALL + 1)
            pool.wait_ge(s_blank, 16 * NT)
            pool.wait_ge(s_slot, 1)
            for b in range(NB):
                for k in range(TOP):
                    pool.indirect_dma_start(routed[:, :], bass.IndirectOffsetOnAxis(ap=slot[0:J, k, b:b + 1], axis=0),
                                            zs[0:J, b, :], None).then_inc(s_scat, 16)

            pool.wait_ge(s_init, 16)
            for t in range(NT):
                p = t % 2
                pool.wait_ge(s_o, t + 1)
                if t:
                    pool.wait_ge(s_added, 16 * t)
                pool.indirect_dma_start(out[:, :], bass.IndirectOffsetOnAxis(ap=token[:, p:p + 1], axis=0),
                                        scaled[:, p, :], None, compute_op=ALU.add).then_inc(s_added, 16)

            pool.wait_ge(s_added, 16 * NT)


        @block.scalar
        def _(act):
            act.wait_ge(s_var, 1)
            act.wait_ge(s_pool, POOL_FIRST)
            nc.scalar.activation(std[0:J, :], mv[0:J, :, 1], ACT.Sqrt, bias=eps[0:J, :]).then_inc(s_std, 1)
            for h in range(2):
                for c in range(HC):
                    act.wait_ge(s_tr, HC * h + c + 1)
                    nc.scalar.activation(xT[:, c, G * h:G * h + G, :],
                                         bank[2 * c + h][:, 0:G * J].rearrange("p (b j) -> p b j", b=G),
                                         ACT.Copy, scale=-2.0).then_inc(s_trc, 1)

            def row_norms(c):
                act.wait_ge(s_cn[c], 16)
                for b in range(NB):
                    if c + b:
                        act.wait_ge(s_aa, c * NB + b)
                    nc.scalar.activation(sq[0:ROWS[c], :], ctxn[0:ROWS[c], c, b, :], ACT.Square,
                                         accum_out=aa[0:ROWS[c], c, b:b + 1]).then_inc(s_aa, 1)

            row_norms(0)
            for c in range(NC):
                if c + 1 < NC:
                    row_norms(c + 1)
                for h in range(2):
                    act.wait_ge(s_sqd, 2 * c + h + 1)
                    v = stage[0:ROWS[c], c, G * h:G * h + G, :]
                    nc.scalar.activation(v, v, ACT.Sqrt).then_inc(s_dist, 1)
                act.wait_ge(s_dist, 2 * c + 2)
                if c == NC - 1:
                    act.wait_ge(s_pool, POOL_EARLY)
                nr = BLOCKS[c] * BR
                act.dma_start(rows_out[c * CR:c * CR + nr, :, :], stage[0:nr, c, :, :]).then_inc(s_rows[c], 16)
            for s0, s1 in COPIES:
                act.wait_ge(s_back, W - s0)
                nc.scalar.activation(big[:, :, s0:s1].rearrange("p r w -> p w r"),
                                     trail[:, s0:s1, 2:2 * BR + 1:2][:, :, ::-1],
                                     ACT.Copy).then_inc(s_path, 1)
            for c in reversed(range(NC)):
                nr = BLOCKS[c] * BR
                act.wait_ge(s_prow[c], 16 * BLOCKS[c])
                act.dma_start(stage[0:nr, c, :, :], rows_back[c * CR:c * CR + nr, :, :]).then_inc(s_unskew[c], 16)
            for n in range(3):
                for g in range(2):
                    act.wait_ge(s_var, 2 + 2 * n + g)
                    nc.scalar.activation(std[0:J, G * g:G * g + G], mv[0:J, G * g:G * g + G, 1],
                                         ACT.Sqrt, bias=eps[0:J, :]).then_inc(s_std, 1)
                if n == 1:
                    act.wait_ge(s_small, 48)
                if n >= 1:
                    for b in range(NB):
                        act.wait_ge(s_tr, 4 + (n - 1) * NB + b + 1)
                        if n == 2:
                            act.wait_ge(s_att, NB)
                        for c in range(HC):
                            last = nc.scalar.activation(xT[:, c, b, :], bank[2 + b % 2][:, c * J:(c + 1) * J],
                                                        ACT.Identity, scale=ln_w[:, 2 * n - 2, c:c + 1],
                                                        bias=ln_w[:, 2 * n - 1, c:c + 1])
                        last.then_inc(s_trc, 1)
            act.wait_ge(s_dif, 1)
            nc.scalar.activation(tops[0:J, :, :], tops[0:J, :, :], ACT.Sigmoid).then_inc(s_sig, 1)

            def silu(n, q):
                act.wait_ge(s_gu, n + 1)
                if not isinstance(n, int) or n >= 2:
                    act.wait_ge(s_hid, n - 1)
                nc.scalar.activation(act_g[:, q, :], bank[q][:, :], ACT.Silu).then_inc(s_silu, 1)

            def copy_hidden(n, q):
                act.wait_ge(s_ht, n + 1)
                if not isinstance(n, int) or n >= 2:
                    act.wait_ge(s_down, n)
                nc.scalar.activation(hidT[:, q, :, :], bank[4 + q][:, :].rearrange("p (f j) -> p f j", f=4),
                                     ACT.Copy).then_inc(s_htc, 1)

            def row_copy(t, p):
                act.wait_ge(s_tiles, t + 1)
                if not isinstance(t, int) or t >= 2:
                    act.wait_ge(s_in_t, t - 1)
                nc.scalar.activation(row_in[:, p, :], rows[:, bass.ds(t, 1), 0:H].rearrange("p a h -> p (a h)"),
                                     ACT.Copy).then_inc(s_rin, 1)

            def tile(t, p):
                row_copy(t + 1, 1 - p)
                silu(2 * t + 1, 1)
                copy_hidden(2 * t, 0)
                silu(2 * t + 2, 0)
                copy_hidden(2 * t + 1, 1)

            row_copy(0, 0)
            silu(0, 0)
            tile(0, 0)
            with act.Fori(0, (NT - 2) // 2) as i:
                tile(2 * i + 1, 1)
                tile(2 * i + 2, 0)
            silu(2 * NT - 1, 1)
            copy_hidden(2 * NT - 2, 0)
            copy_hidden(2 * NT - 1, 1)

        @block.vector
        def _(dve):
            done = [0]

            def link(ins):
                done[0] += 1
                ins.then_inc(s_v, 1)
                dve.wait_ge(s_v, done[0])

            def stats(g0, g1):
                for b in range(g0, g1):
                    last = nc.vector.bn_stats(out=bn6[0:J, b, :], in_=xs_of[b])
                link(last)
                for b in range(g0, g1):
                    last = nc.vector.bn_aggr(out=mv[0:J, b, :], in_=bn6[0:J, b, :])
                last.then_inc(s_var, 1)

            dve.wait_ge(s_x, 16)
            xs_of = [xs[0:J, b, :] for b in range(NB)]
            stats(0, NB)
            dve.wait_ge(s_std, 1)
            dve.wait_ge(s_var, 1)
            link(nc.vector.reciprocal(rstd[0:J, :], std[0:J, :]))
            for b in range(NB):
                nc.vector.tensor_scalar(xn[0:J, b, :], xs[0:J, b, :], mv[0:J, b, 0:1], rstd[0:J, b:b + 1],
                                        ALU.subtract, ALU.mult).then_inc(s_norm, 1)
            for h in range(2):
                for c in range(HC):
                    dve.wait_ge(s_trc, HC * h + c + 1)
                    v = xT[:, c, G * h:G * h + G, :]
                    nc.vector.tensor_tensor(xsq[:, c, G * h:G * h + G, :], v, v, ALU.mult).then_inc(s_xsq, 1)
            dve.wait_ge(s_pool, POOL_EARLY)
            for n in range(2 * NC):
                c, h = n // 2, n % 2
                dve.wait_ge(s_dot, n + 1)
                if c == 0:
                    dve.wait_ge(s_bb, h + 1)
                    link(nc.vector.tensor_copy(bb[:, h, :], bank[h][0:CR, 0:G * J]))
                dve.wait_ge(s_aa, NB * (c + 1))
                for b in range(G * h, G * h + G):
                    o = slice((b % G) * J, (b % G + 1) * J)
                    last = nc.vector.scalar_tensor_tensor(stage[0:ROWS[c], c, b, :], bank[D_BANK[n % 6]][0:ROWS[c], o],
                                                          aa[0:ROWS[c], c, b:b + 1], bb[0:ROWS[c], h, o],
                                                          ALU.add, ALU.add)
                link(last)
                v = stage[0:ROWS[c], c, G * h:G * h + G, :]
                nc.vector.tensor_scalar(v, v, 0.0, None, ALU.max).then_inc(s_sqd, 1)
            dve.wait_ge(s_pool, POOL_EARLY)
            nc.vector.memset(seed[:, :], 0.0)
            nc.vector.tensor_reduce(first[:, 0:1], ident[:, 0:128:KB], AX_X, ALU.add)
            link(nc.vector.tensor_reduce(first[:, 1:2], ident[:, END_K:128:KB], AX_X, ALU.add))
            nc.vector.tensor_scalar(cost[:, 0, 0:1], first[:, 0:1], -BIG, BIG, ALU.mult, ALU.add)
            at = 2 * (BR - 1 - END_R) + 1
            link(nc.vector.tensor_copy(seed[:, at:at + 1], first[:, 1:2]))
            for s in range(W):
                if s % CB == 0 and s // CB < NC:
                    dve.wait_ge(s_skew[s // CB], 16 * BLOCKS[s // CB])
                nc.vector.stream_shuffle(cost[:, s + 1, 0:1], cost[:, s, BR:BR + 1],
                                         [(p & 16) | ((p - 1) & 15) for p in range(32)]).then_inc(s_v, 1)
                nc.vector.tensor_tensor(best[:, s % 2, :], cost[:, s, 0:BR], cost[:, s, 1:BR + 1], ALU.min).then_inc(s_v, 1)
                done[0] += 2
                dve.wait_ge(s_v, done[0])
                link(nc.vector.tensor_tensor_scan(cost[:, s + 1, 1:BR + 1], best[:, s % 2, :], big[:, :, s],
                                                  cost[:, s + 1, 0:1], ALU.min, ALU.add))
            dve.wait_ge(s_pool, POOL_ALL)
            up_c, dg_c, lf_c = cost[:, 1:W + 1, 0:BR], cost[:, 0:W, 0:BR], cost[:, 0:W, 1:BR + 1]
            up_o = ups[:, 0:W, BR:0:-1, 0]
            dg_o = goes[:, 0:W, BR:0:-1, 0]
            lf_o = goes[:, 0:W, BR - 1::-1, 1]
            least = big[:, :, :].rearrange("p r w -> p (r w)").rearrange("p (w r) -> p w r", r=BR)
            link(nc.vector.tensor_tensor(least, up_c, lf_c, ALU.min))
            nc.vector.tensor_tensor(up_o, up_c, lf_c, ALU.is_le)
            link(nc.vector.tensor_tensor(dg_o, dg_c, least, ALU.is_le))
            link(nc.vector.tensor_tensor(up_o, dg_o, up_o, ALU.is_lt))
            link(nc.vector.tensor_tensor(lf_o, dg_o, up_o, ALU.is_equal))
            down = [(p & 16) | min((p & 15) + 1, 15) for p in range(32)]
            for m in (ups, goes):
                link(nc.vector.stream_shuffle(m[:, 0:W - 1, 0, 0], m[:, 1:W, BR, 0], down))
            step0 = step_in[:, 0, :]
            nc.vector.memset(trail[:, W - 1, 0:1], 0.0)
            link(nc.vector.tensor_copy(step0, seed[:, :]))
            for s in reversed(range(W)):
                if s < W - 1:
                    nc.vector.stream_shuffle(trail[:, s, 0:1], trail[:, s + 1, 2 * BR:2 * BR + 1], down).then_inc(s_v, 1)
                    t = trail[:, s + 1, 0:2]
                    pair = bass.AP(tensor=t.tensor, offset=t.offset, ap=[list(t.ap[0]), [2, BR], [2, 2]])
                    nc.vector.tensor_tensor(step0.rearrange("p (r t) -> p r t", t=2), pair,
                                            goes[:, s + 1, 0:BR, :], ALU.mult).then_inc(s_v, 1)
                    done[0] += 2
                    dve.wait_ge(s_v, done[0])
                nc.vector.tensor_tensor_scan(trail[:, s, 1:2 * BR + 1],
                                             ups[:, s, 0:BR, :].rearrange("p r t -> p (r t)"), step0,
                                             trail[:, s, 0:1], ALU.mult, ALU.add).then_inc(s_back, 1)
                dve.wait_ge(s_back, W - s)

            for b in range(NB):
                dve.wait_ge(s_exp, b + 1)
                nc.vector.tensor_tensor(xs[0:J, b, :], xs[0:J, b, :], bank[b][0:J, 0:H], ALU.add).then_inc(s_x2, 1)
            srcs = [xs, xn, xn]
            for n in range(3):
                if n == 2:
                    for b in range(NB):
                        dve.wait_ge(s_att, b + 1)
                        dve.wait_ge(s_y, b + 1)
                        nc.vector.tensor_tensor(hs[0:J, b, :], xn[0:J, b, :], bank[4 + b % 2][0:J, 0:H],
                                                ALU.add).then_inc(s_h, 1)
                src = [xs, xn, hs][n]
                dst = [xn, zs, zs][n]
                up = [s_y, s_z, s_t][n]
                got = [s_x2, s_y, s_h][n]
                xs_of = [src[0:J, b, :] for b in range(NB)]
                dve.wait_ge(got, NB)
                if n:
                    dve.wait_ge([None, s_y, s_z][n], NB)
                for g in range(2):
                    stats(G * g, G * g + G)
                    dve.wait_ge(s_std, 2 + 2 * n + g)
                    dve.wait_ge(s_var, 2 + 2 * n + g)
                    link(nc.vector.reciprocal(rstd[0:J, G * g:G * g + G], std[0:J, G * g:G * g + G]))
                    for b in range(G * g, G * g + G):
                        if n == 2:
                            dve.wait_ge(s_tr, 4 + b + 1)
                        nc.vector.tensor_scalar(dst[0:J, b, 0:H], src[0:J, b, :], mv[0:J, b, 0:1], rstd[0:J, b:b + 1],
                                                ALU.subtract, ALU.mult).then_inc(up, 1)
            for b in range(NB):
                last = nc.vector.tensor_tensor(xs[0:J, b, :], xs[0:J, b, :], hs[0:J, b, :], ALU.add)
            last.then_inc(s_sum, 1)
            dve.wait_ge(s_log, NB)
            link(nc.vector.tensor_copy(logit[0:J, :, :], bank[6][0:J, 0:NB * NE].rearrange("p (b e) -> p b e", b=NB)))
            for b in range(NB):
                last = nc.vector.max(out=top[0:J, b, :], in_=logit[0:J, b, :])
            link(last)
            for b in range(NB):
                nc.vector.max_index(out=topi[0:J, b, :], in_max=top[0:J, b, :], in_values=logit[0:J, b, :])
            nc.vector.tensor_tensor(tops[0:J, :, 0], top[0:J, :, 0], top[0:J, :, 1], ALU.subtract)
            nc.vector.tensor_tensor(tops[0:J, :, 1], top[0:J, :, 1], top[0:J, :, 0], ALU.subtract).then_inc(s_dif, 1)
            dve.wait_ge(s_dif, 1)
            link(nc.vector.tensor_copy(topf[0:J, :, :], topi[0:J, :, 0:2]))
            for k in range(TOP):
                last = nc.vector.tensor_tensor(picked[0:J, k, :, :], iota_e[0:J, :].unsqueeze(1).to_broadcast([J, NB, NE]),
                                               topf[0:J, :, k:k + 1].to_broadcast([J, NB, NE]), ALU.is_equal)
            link(last)
            nc.vector.tensor_tensor(chosen[0:J, :, :], picked[0:J, 0, :, :], picked[0:J, 1, :, :],
                                    ALU.add).then_inc(s_pick, 1)
            nc.vector.tensor_copy(zs[0:J, :, E1], topf[0:J, :, 0])
            dve.wait_ge(s_sig, 1)
            nc.vector.tensor_copy(zs[0:J, :, W2], tops[0:J, :, 1])
            nc.vector.tensor_tensor(zs[0:J, :, WD], tops[0:J, :, 0], tops[0:J, :, 1], ALU.subtract)
            dve.wait_ge(s_rank, 1)
            link(nc.vector.tensor_copy(count[:, :], bank[7][:, NB * NE:NB * NE + NE]))
            link(nc.vector.tensor_tensor(more[:, :, :], count[:, :].unsqueeze(2).to_broadcast([128, NE, MT]),
                                         steps[:, :].unsqueeze(1).to_broadcast([128, NE, MT]), ALU.is_gt))
            link(nc.vector.tensor_reduce(tiles[:, :], more[:, :, :], AX_X, ALU.add))
            link(nc.vector.tensor_tensor_scan(ends[:, :], tiles[:, :], zero8[:, :], 0.0, ALU.add, ALU.add))
            link(nc.vector.tensor_tensor(base[:, :], ends[:, :], tiles[:, :], ALU.subtract))
            link(nc.vector.tensor_scalar(base[:, :], base[:, :], float(ST), None, ALU.mult))
            link(nc.vector.tensor_tensor(place[0:J, :, :], bank[7][0:J, 0:NB * NE].rearrange("p (b e) -> p b e", b=NB),
                                         base[0:J, :].unsqueeze(1).to_broadcast([J, NB, NE]), ALU.add))
            for k in range(TOP):
                last = nc.vector.tensor_tensor(hit[0:J, k, :, :], picked[0:J, k, :, :], place[0:J, :, :], ALU.mult)
            link(last)
            link(nc.vector.tensor_reduce(placef[0:J, :, :], hit[0:J, :, :, :], AX_X, ALU.add))
            nc.vector.tensor_copy(slot[0:J, :, :], placef[0:J, :, :]).then_inc(s_slot, 1)
            link(nc.vector.tensor_tensor(passed[:, :, :], ends[:, :].unsqueeze(1).to_broadcast([128, NT, NE]),
                                         tile_no[:, :].unsqueeze(2).to_broadcast([128, NT, NE]), ALU.is_le))
            link(nc.vector.tensor_reduce(tile_e[:, :], passed[:, :, :], AX_X, ALU.add))
            link(nc.vector.tensor_scalar(tile_e[:, :], tile_e[:, :], float(NE - 1), None, ALU.min))
            nc.vector.tensor_scalar(wrap[:, 0, :], tile_e[:, :], float(RING), -float(RING), ALU.is_ge, ALU.mult)
            link(nc.vector.tensor_scalar(wrap[:, 1, :], tile_e[:, :], float(2 * RING), -float(RING), ALU.is_ge, ALU.mult))
            link(nc.vector.tensor_tensor(wrap[:, 0, :], wrap[:, 0, :], wrap[:, 1, :], ALU.add))
            link(nc.vector.tensor_tensor(tile_w[:, :], wrap[:, 0, :], tile_e[:, :], ALU.add))
            nc.vector.tensor_scalar(table[:, 1, :], tile_w[0:1, :], float(EW), None, ALU.mult)
            nc.vector.tensor_copy(table[:, 0, :], tile_e[0:1, :])
            nc.vector.tensor_copy(ends_i[:, :], ends[0:1, :]).then_inc(s_table, 1)

            def inputs(t, p):
                dve.wait_ge(s_in_t, t + 1)
                if not isinstance(t, int) or t >= 2:
                    dve.wait_ge(s_gu, 2 * t - 2)
                for c in range(HC):
                    last = nc.vector.tensor_scalar(tT[:, p, c, :], bank[7][:, c * ST:(c + 1) * ST],
                                                   ln_w[:, 2, c:c + 1], ln_w[:, 3, c:c + 1], ALU.mult, ALU.add)
                last.then_inc(s_in, 1)

            def hidden(n, q):
                dve.wait_ge(s_silu, n + 1)
                if not isinstance(n, int) or n >= 2:
                    dve.wait_ge(s_ht, n - 1)
                nc.vector.tensor_tensor(hid[:, q, :], act_g[:, q, :], bank[2 + q][:, :], ALU.mult).then_inc(s_hid, 1)

            def scale(t, p):
                dve.wait_ge(s_down, 2 * t + 3)
                if not isinstance(t, int) or t >= 2:
                    dve.wait_ge(s_added, 16 * (t - 1))
                nc.vector.tensor_copy(token[:, p:p + 1], rows[:, bass.ds(t, 1), ID])
                nc.vector.tensor_scalar(scaled[:, p, :], bank[6][:, 0:H], slot_w[:, bass.ds(t, 1)], None,
                                        ALU.mult).then_inc(s_o, 1)

            inputs(0, 0)
            hidden(0, 0)
            inputs(1, 1)
            hidden(1, 1)
            hidden(2, 0)
            dve.wait_ge(s_tiles, NT)
            link(nc.vector.tensor_tensor(slot_w[:, :], rows[:, :, E1], tile_e[:, :], ALU.is_equal))
            link(nc.vector.tensor_tensor(slot_w[:, :], rows[:, :, WD], slot_w[:, :], ALU.mult))
            link(nc.vector.tensor_tensor(slot_w[:, :], rows[:, :, W2], slot_w[:, :], ALU.add))

            def tile(t, p):
                inputs(t + 1, 1 - p)
                hidden(2 * t + 1, 1)
                scale(t - 1, 1 - p)
                hidden(2 * t + 2, 0)

            tile(1, 1)
            tile(2, 0)
            with dve.Fori(1, (NT - 2) // 2) as i:
                tile(2 * i + 1, 1)
                tile(2 * i + 2, 0)
            hidden(2 * NT - 1, 1)
            scale(NT - 2, 0)
            scale(NT - 1, 1)

        @block.tensor
        def _(pe):
            pe.wait_ge(s_pool, POOL_FIRST)
            for h in range(2):
                for c in range(HC):
                    for b in range(G * h, G * h + G):
                        pe.wait_ge(s_norm, b + 1)
                        last = nc.tensor.transpose(bank[2 * c + h][:, (b % G) * J:(b % G + 1) * J],
                                                   xn[0:J, b, c * 128:(c + 1) * 128], ident[0:J, 0:J])
                    last.then_inc(s_tr, 1)
            for n in range(2 * NC):
                c, h = n // 2, n % 2
                if h == 0:
                    pe.wait_ge(s_ct[c], 16)
                pe.wait_ge(s_trc, HC * h + HC)
                if n >= 6:
                    pe.wait_ge(s_sqd, n - 5)
                for b in range(G * h, G * h + G):
                    o = bank[D_BANK[n % 6]][0:ROWS[c], (b % G) * J:(b % G + 1) * J]
                    for kc in range(HC):
                        last = nc.tensor.matmul(o, ctxT[c][:, kc, b, :], xT[:, kc, b, :],
                                                start=(kc == 0), stop=(kc == HC - 1))
                last.then_inc(s_dot, 1)
                if c == 0:
                    pe.wait_ge(s_xsq, HC * h + HC)
                    for kc in range(HC):
                        last = nc.tensor.matmul(bank[h][0:CR, 0:G * J], quarter[:, :],
                                                xsq[:, kc, G * h:G * h + G, :].rearrange("p b j -> p (b j)"),
                                                start=(kc == 0), stop=(kc == HC - 1))
                    last.then_inc(s_bb, 1)
            for c in reversed(range(NC)):
                pe.wait_ge(s_unskew[c], 16)
                for b in range(NB):
                    last = nc.tensor.matmul(bank[b][0:J, 0:H], stage[0:ROWS[c], c, b, :], ctxn[0:ROWS[c], c, b, :],
                                            start=(c == NC - 1), stop=(c == 0))
                    if c == 0:
                        last.then_inc(s_exp, 1)

            def turn(n, src_sem):
                for b in range(NB):
                    pe.wait_ge(src_sem, b + 1)
                    if b >= 2:
                        pe.wait_ge(s_trc, 4 + n * NB + b - 1)
                    elif n == 0:
                        pe.wait_ge(s_x2, NB)
                    for c in range(HC):
                        last = nc.tensor.transpose(bank[2 + b % 2][:, c * J:(c + 1) * J],
                                                   zs[0:J, b, c * 128:(c + 1) * 128], ident[0:J, 0:J])
                    last.then_inc(s_tr, 1)

            turn(0, s_z)
            pe.wait_ge(s_small, 48)
            for b in range(NB):
                pe.wait_ge(s_trc, 4 + b + 1)
                if b >= 2:
                    pe.wait_ge(s_h, b - 1)
                for c in range(HC):
                    last = nc.tensor.matmul(bank[4 + b % 2][0:J, 0:H], xT[:, c, b, :], attn_w[:, c, :],
                                            start=(c == 0), stop=(c == HC - 1))
                last.then_inc(s_att, 1)
            turn(1, s_t)
            for b in range(NB):
                pe.wait_ge(s_trc, 4 + NB + b + 1)
                for c in range(HC):
                    last = nc.tensor.matmul(bank[6][0:J, b * NE:(b + 1) * NE], xT[:, c, b, :], gate_w[:, c, :],
                                            start=(c == 0), stop=(c == HC - 1))
                last.then_inc(s_log, 1)

            pe.wait_ge(s_pick, 1)
            chosen_f = chosen[0:J, :, :].rearrange("p b e -> p (b e)")
            nc.tensor.matmul(bank[7][0:J, 0:NB * NE], before[0:J, 0:J], chosen_f, start=True, stop=False)
            for d in range(1, NB):
                nc.tensor.matmul(bank[7][0:J, d * NE:NB * NE], ones[0:J, 0:J], chosen_f[:, 0:(NB - d) * NE],
                                 start=False, stop=(d == NB - 1))
            for b in range(NB):
                last = nc.tensor.matmul(bank[7][:, NB * NE:NB * NE + NE], ones[0:J, :], chosen_f[:, b * NE:(b + 1) * NE],
                                        start=(b == 0), stop=(b == NB - 1))
            last.then_inc(s_rank, 1)
            pe.wait_ge(s_table, 1)
            pe.sem_inc(s_down, 1)

            def expert(t):
                return pe.value_load(table[0:1, 0, bass.ds(t, 1)], min_val=0, max_val=NE - 1)

            def place_of(t):
                return pe.value_load(table[0:1, 1, bass.ds(t, 1)], min_val=0, max_val=(RING - 1) * EW)

            def turn_in(t, p):
                pe.wait_ge(s_rin, t + 1)
                if not isinstance(t, int) or t >= 1:
                    pe.wait_ge(s_in, t)
                for c in range(HC):
                    last = nc.tensor.transpose(bank[7][:, c * ST:(c + 1) * ST],
                                               row_in[:, p, c * 128:(c + 1) * 128],
                                               ident[:, :])
                last.then_inc(s_in_t, 1)

            def gate_up(n, q, p, at):
                if not isinstance(n, int) or n >= 2:
                    pe.wait_ge(s_hid, n - 1)
                for k in range(2):
                    for c in range(HC):
                        nc_o = (k * HC + c) * F + q * 512
                        last = nc.tensor.matmul(bank[2 * k + q][:, :], tT[:, p, c, :], wflat[:, bass.ds(at + nc_o, 512)],
                                                start=(c == 0), stop=(c == HC - 1))
                last.then_inc(s_gu, 1)

            def first_half(t, p):
                e, at = expert(t), place_of(t)
                pe.wait_ge(s_ready, e + 1)
                pe.wait_ge(s_in, t + 1)
                gate_up(2 * t, 0, p, at)

            def turn_hidden(n, q):
                pe.wait_ge(s_hid, n + 1)
                if not isinstance(n, int) or n >= 2:
                    pe.wait_ge(s_htc, n - 1)
                for f in range(4):
                    last = nc.tensor.transpose(bank[4 + q][:, f * ST:(f + 1) * ST], hid[:, q, f * 128:(f + 1) * 128],
                                               ident[:, :])
                last.then_inc(s_ht, 1)

            def down(n, q, t, p, at):
                pe.wait_ge(s_htc, n + 1)
                if q == 0 and (not isinstance(t, int) or t >= 1):
                    pe.wait_ge(s_o, t)
                for f in range(4):
                    o = 2 * HC * F + (4 * q + f) * H
                    last = nc.tensor.matmul(bank[6][:, 0:H], hidT[:, q, f, :],
                                            wflat[:, bass.ds(at + o, H)], start=(q == 0 and f == 0), stop=(q == 1 and f == 3))
                last.then_inc(s_down, 1)

            def tile(t, p):
                here = place_of(t)
                gate_up(2 * t + 1, 1, p, here)
                if not isinstance(t, int) or t < NT - 1:
                    turn_in(t + 1, 1 - p)
                turn_hidden(2 * t, 0)
                if not isinstance(t, int) or t:
                    down(2 * t - 1, 1, t - 1, 1 - p, place_of(t - 1))
                if not isinstance(t, int) or t < NT - 1:
                    first_half(t + 1, 1 - p)
                turn_hidden(2 * t + 1, 1)
                down(2 * t, 0, t, p, here)

            turn_in(0, 0)
            first_half(0, 0)
            tile(0, 0)
            with pe.Fori(0, (NT - 2) // 2) as i:
                tile(2 * i + 1, 1)
                tile(2 * i + 2, 0)
            tile(NT - 1, 1)
            down(2 * NT - 1, 1, NT - 1, 1, place_of(NT - 1))


def kernel(x, ctx_1024, L0_ffn_ln1_g, L0_ffn_ln1_b, L0_ffn_attn_w, L0_ffn_ln2_g, L0_ffn_ln2_b,
           L0_ffn_gate_w, L0_ffn_gate_proj, L0_ffn_up_proj, L0_ffn_down_proj):
    import numpy as np
    import concourse.bacc as bacc
    from concourse.bass_utils import run_bass_kernel_spmd

    def by_partition(a, axis):
        a = np.moveaxis(np.asarray(a), axis, 0)
        return np.moveaxis(a.reshape((a.shape[0] // 128, 128) + a.shape[1:]), 0, 1)

    ctx = np.asarray(ctx_1024)
    ln = np.stack([np.asarray(v) for v in (L0_ffn_ln1_g, L0_ffn_ln1_b, L0_ffn_ln2_g, L0_ffn_ln2_b)])
    laid = {
        "x": np.asarray(x).transpose(1, 0, 2),
        "ctx_t": np.concatenate([by_partition(ctx[:, c * CR:c * CR + ROWS[c]], 2).reshape(128, -1) for c in range(NC)], 1),
        "ctx_n": ctx.transpose(1, 0, 2),
        "ln": by_partition(ln, 1).transpose(0, 2, 1),
        "attn_t": by_partition(L0_ffn_attn_w, 1),
        "gate_t": by_partition(L0_ffn_gate_w, 1),
        "gate_proj": np.stack([by_partition(w, 1) for w in np.asarray(L0_ffn_gate_proj)]).reshape(NE, 128, HC * F),
        "up_proj": np.stack([by_partition(w, 1) for w in np.asarray(L0_ffn_up_proj)]).reshape(NE, 128, HC * F),
        "down_proj": np.stack([by_partition(w, 1) for w in np.asarray(L0_ffn_down_proj)]).reshape(NE, 128, FC * H),
    }
    nc = bacc.Bacc("TRN2", target_bir_lowering=False, num_devices=1)
    arrays, args = {}, []
    for name, a in laid.items():
        arrays[name] = np.ascontiguousarray(a)
        args.append(nc.dram_tensor(name, a.shape, mybir.dt.from_np(a.dtype), kind="ExternalInput").ap())
    args.append(nc.dram_tensor("out", (NB * J + ST, H), F32, kind="ExternalOutput").ap())
    align_and_route(nc, *args)
    got = run_bass_kernel_spmd(nc, [arrays], core_ids=[0]).results[0]["out"]
    return np.ascontiguousarray(got[0:NB * J].reshape(NB, J, H))
```

```python
from contextlib import ExitStack

import concourse.bass as bass
from concourse import mybir

F32 = mybir.dt.float32
BF16 = mybir.dt.bfloat16
U32 = mybir.dt.uint32
I32 = mybir.dt.int32
ALU = mybir.AluOpType
ACT = mybir.ActivationFunctionType
AX_X = mybir.AxisListType.X

NB = 8
J = 100
NI = 361
H = 256
HC = H // 128
F = 1024
FC = F // 128
NE = 8
BR = 25
KB = 16
NK = -(-NI // BR)
CB = 4
CR = CB * BR
NC = -(-NI // CR)
ROWS = [min(CR, NI - c * CR) for c in range(NC)]
BLOCKS = [min(CB, NK - c * CB) for c in range(NC)]
W = J + NK - 1
END_K, END_R = (NI - 1) // BR, (NI - 1) % BR
GC = 3
G = 4
PG = NB // 2
LAG = [0, 1, 2, 3, 4]
BIG = 1e30
EPS = 1e-5
RING = 3
TOP = 2
ST = 128
NT = (TOP * NB * J + NE * (ST - 1)) // ST
MT = -(-NB * J // ST)
EW = 3 * HC * F


def align_and_route(nc, x, ctx_t, ctx_n, ln, attn_t, gate_t, gate_proj, up_proj, down_proj, out):
    with ExitStack() as stack:
        def sb(name, shape, dt=F32):
            return stack.enter_context(nc.sbuf_tensor(name, shape, dt))

        def sem(name):
            return stack.enter_context(nc.semaphore(name))

        bank = [stack.enter_context(nc.psum_tensor(f"bank{i}", [128, 512], F32)) for i in range(8)]

        rows_out = nc.dram_tensor("distance_rows", (NK * BR, NB, J), F32, kind="Internal").ap()
        rows_back = nc.dram_tensor("path_rows", (NK * BR, NB, J), F32, kind="Internal").ap()
        normed = nc.dram_tensor("normed_rows", (NB * J, H), F32, kind="Internal").ap()

        weights = sb("weights", [128, RING, EW])
        big = sb("big", [128, BR, W])
        cost = sb("cost", [128, W + 1, BR + 1])
        shared = sb("shared", [128, W * (BR + 1) * 2])
        trail = sb("trail", [128, W, 2 * BR + 1], BF16)
        stage = sb("stage", [128, NC, NB, J])
        ctxn = sb("ctxn", [128, NC, NB, H])
        xs = sb("xs", [128, NB, H])
        xn = sb("xn", [128, NB, H])
        xT = sb("xT", [128, HC, NB, J])
        attn_w = sb("attn_w", [128, HC, H])
        gate_w = sb("gate_w", [128, HC, NE])
        ln_w = sb("ln_w", [128, 4, HC])
        ident = sb("ident", [128, 128])
        quarter = sb("quarter", [128, CR])
        seed = sb("seed", [128, 2 * BR], BF16)
        first = sb("first", [128, 2])
        bn6 = sb("bn6", [128, 3, NB, 6])
        mv = sb("mv", [128, 3, NB, 2])
        std = sb("std", [128, 3, NB])
        rstd = sb("rstd", [128, 3, NB])
        shift = sb("shift", [128, 3, NB])
        aa = sb("aa", [128, NC, NB])
        eps = sb("eps", [128, 1])
        best = sb("best", [128, 2, BR])
        step_in = sb("step_in", [128, 2, 2 * BR], BF16)
        top = sb("top", [128, NB, 8])
        topi = sb("topi", [128, NB, 8], U32)
        tops = sb("tops", [128, NB, 2])
        iota_e = sb("iota_e", [128, NE])
        picked = sb("picked", [128, TOP, NB, NE])
        chosen = sb("chosen", [128, NB, NE], BF16)
        before = sb("before", [128, ST], BF16)
        ones = sb("ones", [128, 128], BF16)
        count = sb("count", [128, NE])
        steps = sb("steps", [128, MT])
        more = sb("more", [128, NE, MT])
        tiles = sb("tiles", [128, NE])
        zero8 = sb("zero8", [128, NE])
        ends = sb("ends", [128, NE])
        base = sb("base", [128, NE])
        place = sb("place", [128, NB, NE])
        hit = sb("hit", [128, TOP, NB, NE])
        placef = sb("placef", [128, TOP, NB])
        slot = sb("slot", [128, TOP, NB], U32)
        inner = sb("inner", [128, TOP, NB], U32)
        outer = sb("outer", [128, TOP, NB])
        tile_no = sb("tile_no", [128, NT])
        passed = sb("passed", [128, NT, NE])
        tile_e = sb("tile_e", [128, NT])
        wrap = sb("wrap", [128, 2, NT])
        tile_w = sb("tile_w", [128, NT])
        table = sb("table", [1, 2, NT], I32)
        ends_i = sb("ends_i", [1, NE], I32)
        row_no = sb("row_no", [128, ST])
        tile_first = sb("tile_first", [128, NT])
        batch_at = sb("batch_at", [128, NB])
        row_at = sb("row_at", [128, 1])
        w_rest = sb("w_rest", [128, NB, TOP])
        w_part = sb("w_part", [128, 3, NB, TOP], BF16)
        part = sb("part", [128, 5, NT])
        behind = sb("behind", [128, 1])
        slot_w = sb("slot_w", [128, NT])
        slot_t = sb("slot_t", [128, NT])
        empty = sb("empty", [128, NT])
        fetch = sb("fetch", [128, NT], U32)
        target = sb("target", [128, NT], U32)
        flat = cost[:, :, :].rearrange("p s r -> p (s r)")
        act_g = flat[:, 0:1024].rearrange("p (q f) -> p q f", q=2)
        hid = flat[:, 1024:2048].rearrange("p (q f) -> p q f", q=2)
        row_in = flat[:, 2048:2560].rearrange("p (q h) -> p q h", q=2)
        flat = big[:, :, :].rearrange("p r w -> p (r w)")
        hidT = flat[:, 0:1024].rearrange("p (q f s) -> p q f s", q=2, f=4)
        tT = flat[:, 1024:1536].rearrange("p (q c s) -> p q c s", q=2, c=HC)
        scaled = flat[:, 1536:2048].rearrange("p (q h) -> p q h", q=2)

        ctxT = [shared[:, HC * NB * c * CR:HC * NB * (c * CR + ROWS[c])].rearrange("p (k b r) -> p k b r", k=HC, b=NB)
                for c in range(NC)]
        sq = cost[:, :, :].rearrange("p s r -> p (s r)")[:, 2048:2048 + H]
        xsq = cost[:, :, :].rearrange("p s r -> p (s r)")[:, BR + 1:BR + 1 + HC * NB * J].rearrange(
            "p (c b j) -> p c b j", c=HC, b=NB)
        least = xn[:, :, :].rearrange("p b h -> p (b h)")[:, 1024:1024 + 2 * GC * BR].rearrange(
            "p (q s r) -> p q s r", q=2, s=GC)
        bb = xn[0:CR, :, :].rearrange("p b h -> p (b h)")[:, 0:NB * J].rearrange("p (h n) -> p h n", h=2)
        half = shared[:, :].bitcast(BF16)
        NA = W * (BR + 1) * 2
        ups = half[:, 0:NA].rearrange("p (s r t) -> p s r t", s=W, t=2)
        goes = half[:, NA:2 * NA].rearrange("p (s r t) -> p s r t", s=W, t=2)
        spare = ctxn[:, :, :, :].rearrange("p c b h -> p (c b h)")
        zs = spare[:, 0:NB * H].rearrange("p (b h) -> p b h", b=NB)
        hs = spare[:, NB * H:2 * NB * H].rearrange("p (b h) -> p b h", b=NB)
        n = TOP * NB
        match = half[:, 0:n * ST].rearrange("p (n s) -> p n s", n=n)
        marks = half[:, n * ST:n * (ST + 5 * NT)].rearrange("p (n k t) -> p n k t", n=n, k=5)
        in_tile = half[:, n * (ST + 5 * NT):n * (ST + 6 * NT)].rearrange("p (n t) -> p n t", n=n)
        wflat = weights[:, :, :].rearrange("p r n -> p (r n)")

        s_x = sem("x_loaded")
        s_ct = [sem(f"ctx_t_loaded{c}") for c in range(NC)]
        s_cn = [sem(f"ctx_n_loaded{c}") for c in range(NC)]
        s_small = sem("small_loaded")
        s_w = [sem(f"expert_loaded{i}") for i in range(RING)]
        s_pool = sem("constants_ready")
        s_v = sem("vector_step")
        s_var = sem("variances_ready")
        s_std = sem("std_ready")
        s_norm = sem("normed_ready")
        s_tr = sem("transposed")
        s_trc = sem("transposed_copied")
        s_xsq = sem("squares_of_x")
        s_bb = sem("column_norms_ready")
        s_aa = sem("row_norms_ready")
        s_dot = sem("products_ready")
        s_sqd = sem("squares_ready")
        s_dist = sem("distances_ready")
        s_skew = [sem(f"distances_skewed{c}") for c in range(NC)]
        s_rows = [sem(f"distance_rows_stored{c}") for c in range(NC)]
        s_prow = [sem(f"path_rows_stored{c}") for c in range(NC)]
        s_back = sem("path_steps")
        s_path = sem("path_copied")
        s_unskew = [sem(f"path_staged{c}") for c in range(NC)]
        s_exp = sem("expanded")
        s_x2 = sem("residual_added")
        s_mv = [sem(f"variances{n}") for n in range(3)]
        s_dev = [sem(f"deviations{n}") for n in range(3)]
        s_scale = [None, sem("scales1"), sem("scales2")]
        s_y = sem("second_norm")
        s_z = sem("third_norm")
        s_zt = sem("third_norm_turned")
        s_ztc = sem("third_norm_copied")
        s_att = sem("attn_ready")
        s_h = sem("h_ready")
        s_t = sem("t_ready")
        s_tt = sem("t_turned")
        s_ttc = sem("t_copied")
        s_log = sem("logits_ready")
        s_sum = sem("x_plus_h_ready")
        s_dif = sem("gate_difference")
        s_sig = sem("gate_weights")
        s_gu = sem("gate_up_ready")
        s_silu = sem("silu_ready")
        s_hid = sem("hidden_ready")
        s_ht = sem("hidden_turned")
        s_htc = sem("hidden_copied")
        s_down = sem("down_ready")
        s_o = sem("tile_scaled")
        s_in = sem("tile_inputs_ready")
        s_in_t = sem("tile_inputs_turned")
        s_ready = sem("experts_ready")
        s_rank = sem("ranks_ready")
        s_pick = sem("choices_for_ranks")
        s_match = sem("slots_matched")
        s_heavy = sem("weights_marked")
        s_marks = sem("slots_filled")
        s_index = sem("slot_tokens_ready")
        s_saved = sem("normed_rows_stored")
        s_table = sem("tables_ready")
        s_row = [sem(f"tile_rows_loaded{p}") for p in range(2)]
        s_init = sem("output_started")
        s_added = sem("tile_added")

        block = stack.enter_context(nc.Block())
        POOL_FIRST = 4
        POOL_EARLY = 7
        POOL_ALL = POOL_EARLY + 16
        assert W % GC == 0 and GC == 3
        COPIES = [(76, W), (44, 76), (12, 44), (8, 12), (4, 8), (0, 4)]
        D_BANK = [4, 5, 6, 7, 2, 3]

        @block.sync
        def _(sp):
            sp.dma_start(xs[0:J, :, :], x).then_inc(s_x, 16)
            for c in range(NC):
                n, o = ROWS[c], HC * NB * c * CR
                sp.dma_start(shared[:, o:o + HC * NB * n], ctx_t[:, o:o + HC * NB * n]).then_inc(s_ct[c], 16)
                sp.dma_start(ctxn[0:n, c, :, :], ctx_n[c * CR:c * CR + n, :, :]).then_inc(s_cn[c], 16)
            sp.dma_start(attn_w[:, :, :], attn_t).then_inc(s_small, 16)
            sp.dma_start(gate_w[:, :, :], gate_t).then_inc(s_small, 16)
            sp.dma_start(ln_w[:, :, :], ln).then_inc(s_small, 16)
            sp.wait_ge(s_pool, POOL_EARLY)
            for c in range(NC):
                sp.wait_ge(s_rows[c], 16)
                for k in range(c * CB, c * CB + BLOCKS[c]):
                    sp.dma_start(big[k:128:KB, :, k:k + J],
                                 rows_out[k * BR:(k + 1) * BR, :, :].rearrange("r b j -> b r j")
                                 ).then_inc(s_skew[c], 16)

            def load_expert(e):
                r = weights[:, e % RING, :]
                n = HC * F
                sp.dma_start(r[:, 0:n], gate_proj[e]).then_inc(s_w[e % RING], 16)
                sp.dma_start(r[:, n:2 * n], up_proj[e]).then_inc(s_w[e % RING], 16)
                sp.dma_start(r[:, 2 * n:3 * n], down_proj[e]).then_inc(s_w[e % RING], 16)

            for e in range(RING):
                load_expert(e)
            for n, c in enumerate(reversed(range(NC))):
                sp.wait_ge(s_path, len(COPIES) - NC + 1 + n)
                for k in range(c * CB, c * CB + BLOCKS[c]):
                    sp.dma_start(rows_back[k * BR:(k + 1) * BR, :, :].rearrange("r b j -> b r j"),
                                 big[k:128:KB, :, k:k + J]).then_inc(s_prow[c], 16)
            for e in range(RING):
                sp.wait_ge(s_w[e], 48)
                sp.sem_inc(s_ready, 1)
            sp.wait_ge(s_t, PG)
            sp.dma_start(normed.rearrange("(b j) h -> j b h", b=NB), zs[0:J, :, :]).then_inc(s_saved, 16)
            sp.wait_ge(s_sum, PG)
            sp.dma_start(out[0:NB * J, :].rearrange("(b j) h -> j b h", b=NB), xs[0:J, :, :]).then_inc(s_init, 16)
            sp.wait_ge(s_table, 1)
            for e in range(RING, NE):
                last_tile = sp.value_load(ends_i[0:1, e - RING:e - RING + 1], min_val=0, max_val=NT)
                sp.wait_ge(s_down, last_tile * 2 + 1)
                load_expert(e)
                sp.wait_ge(s_w[e % RING], 48 * (e // RING + 1))
                sp.sem_inc(s_ready, 1)

        @block.gpsimd
        def _(pool):
            pool.memset(ident[:, :], 0.0).then_inc(s_pool, 1)
            pool.memset(eps[:, :], EPS).then_inc(s_pool, 1)
            pool.wait_ge(s_pool, 2)
            pool.affine_select(out=ident[:, :], in_=ident[:, :], compare_op=ALU.not_equal, fill=1.0,
                               base=0, pattern=[[-1, 128]], channel_multiplier=1).then_inc(s_pool, 1)
            pool.memset(quarter[:, :], 0.25).then_inc(s_pool, 1)
            pool.memset(stage[:, NC - 1, :, :], 0.0).then_inc(s_pool, 1)
            pool.memset(big[:, :, :], BIG).then_inc(s_pool, 1)
            pool.memset(cost[:, 0, :], BIG).then_inc(s_pool, 1)
            pool.iota(iota_e[:, :], pattern=[[1, NE]], base=0, channel_multiplier=0,
                      allow_small_or_imprecise_dtypes=True).then_inc(s_pool, 1)
            pool.iota(steps[:, :], pattern=[[ST, MT]], base=0, channel_multiplier=0,
                      allow_small_or_imprecise_dtypes=True).then_inc(s_pool, 1)
            pool.iota(tile_no[:, :], pattern=[[1, NT]], base=0, channel_multiplier=0,
                      allow_small_or_imprecise_dtypes=True).then_inc(s_pool, 1)
            pool.memset(zero8[:, :], 0.0).then_inc(s_pool, 1)
            pool.memset(ones[:, :], 1.0).then_inc(s_pool, 1)
            pool.memset(before[:, :], 1.0).then_inc(s_pool, 1)
            pool.iota(row_no[:, :], pattern=[[1, ST]], base=0, channel_multiplier=0,
                      allow_small_or_imprecise_dtypes=True).then_inc(s_pool, 1)
            pool.wait_ge(s_pool, POOL_EARLY + 2)
            pool.memset(steps[:, 0:1], -1.0).then_inc(s_pool, 1)
            pool.iota(tile_first[:, :], pattern=[[ST, NT]], base=0, channel_multiplier=0,
                      allow_small_or_imprecise_dtypes=True).then_inc(s_pool, 1)
            pool.iota(batch_at[:, :], pattern=[[J, NB]], base=0, channel_multiplier=0,
                      allow_small_or_imprecise_dtypes=True).then_inc(s_pool, 1)
            pool.iota(row_at[:, :], pattern=[[0, 1]], base=1, channel_multiplier=1,
                      allow_small_or_imprecise_dtypes=True).then_inc(s_pool, 1)
            pool.iota(behind[:, :], pattern=[[0, 1]], base=NB * J + 1, channel_multiplier=1,
                      allow_small_or_imprecise_dtypes=True).then_inc(s_pool, 1)
            pool.wait_ge(s_pool, POOL_EARLY + 12)
            pool.affine_select(out=before[:, :], in_=before[:, :], compare_op=ALU.is_gt, fill=0.0,
                               base=0, pattern=[[1, ST]], channel_multiplier=-1).then_inc(s_pool, 1)
            for c in range(NC):
                pool.wait_ge(s_dist, 2 * c + 2)
                nr = BLOCKS[c] * BR
                pool.dma_start(rows_out[c * CR:c * CR + nr, :, :], stage[0:nr, c, :, :]).then_inc(s_rows[c], 16)
            pool.wait_ge(s_dot, 2 * NC)
            pool.memset(ups[:, :, :, 1], 1.0).then_inc(s_pool, 1)
            pool.memset(ups[:, W - 1, 0, 0:1], 0.0).then_inc(s_pool, 1)
            pool.memset(goes[:, W - 1, 0, 0:1], 0.0).then_inc(s_pool, 1)
            for g in range(PG):
                pool.wait_ge(s_h, g + 1)
                pool.tensor_tensor(xs[0:J, 2 * g:2 * g + 2, :], xs[0:J, 2 * g:2 * g + 2, :],
                                   hs[0:J, 2 * g:2 * g + 2, :], ALU.add).then_inc(s_sum, 1)

            def fetch_rows(t):
                if t >= 2:
                    pool.wait_ge(s_in_t, t - 1)
                pool.indirect_dma_start(row_in[:, t % 2, :], None, normed[:, :],
                                        bass.IndirectOffsetOnAxis(ap=fetch[:, t:t + 1], axis=0)
                                        ).then_inc(s_row[t % 2], 16)

            pool.wait_ge(s_saved, 16)
            pool.wait_ge(s_index, 1)
            for t in range(4):
                fetch_rows(t)
            pool.wait_ge(s_init, 16)
            pool.wait_ge(s_index, 2)
            pool.wait_ge(s_table, 1)
            used = pool.value_load(ends_i[0:1, NE - 1:NE], min_val=NE, max_val=NT)

            def add_rows(t):
                pool.wait_ge(s_o, t + 1)
                if t:
                    pool.wait_ge(s_added, 16 * t)
                pool.indirect_dma_start(out[:, :], bass.IndirectOffsetOnAxis(ap=target[:, t:t + 1], axis=0),
                                        scaled[:, t % 2, :], None, compute_op=ALU.add).then_inc(s_added, 16)

            for t in range(NE - 4):
                fetch_rows(t + 4)
                add_rows(t)
            for t in range(NE - 4, NT):
                if t + 4 < NT:
                    with pool.If(used > t + 4):
                        fetch_rows(t + 4)
                if t < NE:
                    add_rows(t)
                else:
                    with pool.If(used > t):
                        add_rows(t)
            pool.wait_ge(s_added, used * 16)

        @block.scalar
        def _(act):
            act.wait_ge(s_var, 1)
            act.wait_ge(s_pool, POOL_FIRST)
            nc.scalar.activation(std[0:J, 0, :], mv[0:J, 0, :, 1], ACT.Sqrt, bias=eps[0:J, :]).then_inc(s_std, 1)
            for h in range(2):
                for c in range(HC):
                    act.wait_ge(s_tr, HC * h + c + 1)
                    nc.scalar.activation(xT[:, c, G * h:G * h + G, :],
                                         bank[2 * c + h][:, 0:G * J].rearrange("p (b j) -> p b j", b=G),
                                         ACT.Copy, scale=-2.0).then_inc(s_trc, 1)

            def row_norms(c):
                act.wait_ge(s_cn[c], 16)
                for b in range(NB):
                    if c + b:
                        act.wait_ge(s_aa, c * NB + b)
                    nc.scalar.activation(sq[0:ROWS[c], :], ctxn[0:ROWS[c], c, b, :], ACT.Square,
                                         accum_out=aa[0:ROWS[c], c, b:b + 1]).then_inc(s_aa, 1)

            row_norms(0)
            for c in range(NC):
                if c + 1 < NC - 1:
                    row_norms(c + 1)
                for h in range(2):
                    act.wait_ge(s_sqd, 2 * c + h + 1)
                    v = stage[0:ROWS[c], c, G * h:G * h + G, :]
                    nc.scalar.activation(v, v, ACT.Sqrt).then_inc(s_dist, 1)

            def stage_path(c):
                act.wait_ge(s_prow[c], 16 * BLOCKS[c])
                nr = BLOCKS[c] * BR
                act.dma_start(stage[0:nr, c, :, :], rows_back[c * CR:c * CR + nr, :, :]).then_inc(s_unskew[c], 16)

            for s0, s1 in COPIES:
                if s0 == 0:
                    stage_path(NC - 1)
                act.wait_ge(s_back, W - s0)
                nc.scalar.activation(big[:, :, s0:s1].rearrange("p r w -> p w r"),
                                     trail[:, s0:s1, 2:2 * BR + 1:2][:, :, ::-1],
                                     ACT.Copy).then_inc(s_path, 1)
            for c in reversed(range(NC - 1)):
                stage_path(c)

            def deviation(n, g):
                act.wait_ge(s_mv[n], g + 1)
                nc.scalar.activation(std[0:J, n, 2 * g:2 * g + 2], mv[0:J, n, 2 * g:2 * g + 2, 1],
                                     ACT.Sqrt, bias=eps[0:J, :]).then_inc(s_dev[n], 1)

            def norm(n, g, src, ready):
                act.wait_ge(s_scale[n], g + 1)
                for b in (2 * g, 2 * g + 1):
                    last = nc.scalar.activation(zs[0:J, b, :], src[0:J, b, :], ACT.Identity,
                                                scale=rstd[0:J, n, b:b + 1], bias=shift[0:J, n, b:b + 1])
                last.then_inc(ready, 1)

            def copy_turned(g, first_bank, gain, turned, copied):
                act.wait_ge(turned, g + 1)
                for c in range(HC):
                    last = nc.scalar.activation(xT[:, c, 2 * g:2 * g + 2, :],
                                                bank[first_bank + g % 2][:, 2 * c * J:2 * (c + 1) * J].rearrange(
                                                    "p (b j) -> p b j", b=2),
                                                ACT.Identity, scale=ln_w[:, gain, c:c + 1],
                                                bias=ln_w[:, gain + 1, c:c + 1])
                last.then_inc(copied, 1)

            act.wait_ge(s_small, 48)
            for turn in range(1, PG + 4):
                g1, g2, g3 = turn - 1, turn - 2, turn - 4
                if g1 < PG:
                    deviation(0, g1)
                if 0 <= g2 < PG:
                    deviation(1, g2)
                if 0 <= g3 < PG:
                    deviation(2, g3)
                if 0 <= g2 < PG:
                    if g2 == 0:
                        act.wait_ge(s_exp, PG)
                    norm(1, g2, xn, s_z)
                if 0 <= g3 < PG:
                    act.wait_ge(s_zt, g3 + 1)
                    norm(2, g3, hs, s_t)
                if 0 <= g2 < PG:
                    copy_turned(g2, 0, 0, s_zt, s_ztc)
                if 0 <= g3 < PG:
                    act.wait_ge(s_att, g3 + 1)
                    copy_turned(g3, 2, 2, s_tt, s_ttc)
            act.wait_ge(s_dif, 1)
            nc.scalar.activation(tops[0:J, :, :], tops[0:J, :, :], ACT.Sigmoid).then_inc(s_sig, 1)

            def silu(n, q):
                act.wait_ge(s_gu, n + 1)
                if not isinstance(n, int) or n >= 2:
                    act.wait_ge(s_hid, n - 1)
                nc.scalar.activation(act_g[:, q, :], bank[q][:, :], ACT.Silu).then_inc(s_silu, 1)

            def copy_hidden(n, q):
                act.wait_ge(s_ht, n + 1)
                if not isinstance(n, int) or n >= 2:
                    act.wait_ge(s_down, n)
                nc.scalar.activation(hidT[:, q, :, :], bank[4 + q][:, :].rearrange("p (f j) -> p f j", f=4),
                                     ACT.Copy).then_inc(s_htc, 1)

            act.wait_ge(s_table, 1)
            used = act.value_load(ends_i[0:1, NE - 1:NE], min_val=NE, max_val=NT)

            def tile(t, p):
                with act.If(t < used):
                    silu(2 * t + 1, 1)
                    copy_hidden(2 * t, 0)
                    with act.If(t + 1 < used):
                        silu(2 * t + 2, 0)
                    copy_hidden(2 * t + 1, 1)

            silu(0, 0)
            silu(1, 1)
            copy_hidden(0, 0)
            silu(2, 0)
            copy_hidden(1, 1)
            with act.Fori(0, (NT - 2) // 2) as i:
                tile(2 * i + 1, 1)
                tile(2 * i + 2, 0)
            with act.If(used > NT - 1):
                silu(2 * NT - 1, 1)
                copy_hidden(2 * NT - 2, 0)
                copy_hidden(2 * NT - 1, 1)

        @block.vector
        def _(dve):
            done = [0]

            def link(ins):
                done[0] += 1
                ins.then_inc(s_v, 1)
                dve.wait_ge(s_v, done[0])

            dve.wait_ge(s_x, 16)
            for b in range(NB):
                last = nc.vector.bn_stats(out=bn6[0:J, 0, b, :], in_=xs[0:J, b, :])
            link(last)
            for b in range(NB):
                last = nc.vector.bn_aggr(out=mv[0:J, 0, b, :], in_=bn6[0:J, 0, b, :])
            last.then_inc(s_var, 1)
            dve.wait_ge(s_std, 1)
            dve.wait_ge(s_var, 1)
            link(nc.vector.reciprocal(rstd[0:J, 0, :], std[0:J, 0, :]))
            for b in range(NB):
                nc.vector.tensor_scalar(xn[0:J, b, :], xs[0:J, b, :], mv[0:J, 0, b, 0:1], rstd[0:J, 0, b:b + 1],
                                        ALU.subtract, ALU.mult).then_inc(s_norm, 1)
            for h in range(2):
                for c in range(HC):
                    dve.wait_ge(s_trc, HC * h + c + 1)
                    v = xT[:, c, G * h:G * h + G, :]
                    nc.vector.tensor_tensor(xsq[:, c, G * h:G * h + G, :], v, v, ALU.mult).then_inc(s_xsq, 1)
            dve.wait_ge(s_pool, POOL_EARLY)
            nc.vector.memset(seed[:, :], 0.0)
            nc.vector.tensor_reduce(first[:, 0:1], ident[:, 0:128:KB], AX_X, ALU.add)
            link(nc.vector.tensor_reduce(first[:, 1:2], ident[:, END_K:128:KB], AX_X, ALU.add))
            nc.vector.tensor_scalar(cost[:, 0, 0:1], first[:, 0:1], -BIG, BIG, ALU.mult, ALU.add)
            at = 2 * (BR - 1 - END_R) + 1
            link(nc.vector.tensor_copy(seed[:, at:at + 1], first[:, 1:2]))
            for n in range(2 * NC):
                c, h = n // 2, n % 2
                if n == 2 * NC - 4:
                    r = ROWS[NC - 1]
                    dve.wait_ge(s_cn[NC - 1], 16)
                    for b in range(NB):
                        last = nc.vector.scalar_tensor_tensor(weights[0:r, RING - 1, b * H:(b + 1) * H],
                                                              ctxn[0:r, NC - 1, b, :], 1.0, ctxn[0:r, NC - 1, b, :],
                                                              ALU.mult, ALU.mult, accum_out=aa[0:r, NC - 1, b:b + 1])
                    link(last)
                dve.wait_ge(s_dot, n + 1)
                if c == 0:
                    dve.wait_ge(s_bb, h + 1)
                    link(nc.vector.tensor_copy(bb[:, h, :], bank[h][0:CR, 0:G * J]))
                if c < NC - 1:
                    dve.wait_ge(s_aa, NB * (c + 1))
                for b in range(G * h, G * h + G):
                    o = slice((b % G) * J, (b % G + 1) * J)
                    last = nc.vector.scalar_tensor_tensor(stage[0:ROWS[c], c, b, :], bank[D_BANK[n % 6]][0:ROWS[c], o],
                                                          aa[0:ROWS[c], c, b:b + 1], bb[0:ROWS[c], h, o],
                                                          ALU.add, ALU.add)
                link(last)
                v = stage[0:ROWS[c], c, G * h:G * h + G, :]
                nc.vector.tensor_scalar(v, v, 0.0, None, ALU.max).then_inc(s_sqd, 1)

            def choice(s, stage_of):
                up_c = cost[:, s + 1:s + 1 + GC, 0:BR]
                dg_c, lf_c = cost[:, s:s + GC, 0:BR], cost[:, s:s + GC, 1:BR + 1]
                up_o = ups[:, s:s + GC, BR:0:-1, 0]
                dg_o, lf_o = goes[:, s:s + GC, BR:0:-1, 0], goes[:, s:s + GC, BR - 1::-1, 1]
                low = least[:, s // GC % 2, :, :]
                ins = [(low, up_c, lf_c, ALU.min), (up_o, up_c, lf_c, ALU.is_le), (dg_o, dg_c, low, ALU.is_le),
                       (up_o, dg_o, up_o, ALU.is_lt), (lf_o, dg_o, up_o, ALU.is_equal)][stage_of]
                nc.vector.tensor_tensor(*ins).then_inc(s_v, 1)
                done[0] += 1
                return done[0]

            dve.wait_ge(s_dot, 2 * NC)
            made = {}
            for s in range(W):
                if s % CB == 0 and s // CB < NC:
                    dve.wait_ge(s_skew[s // CB], 16 * BLOCKS[s // CB])
                nc.vector.stream_shuffle(cost[:, s + 1, 0:1], cost[:, s, BR:BR + 1],
                                         [(p & 16) | ((p - 1) & 15) for p in range(32)]).then_inc(s_v, 1)
                nc.vector.tensor_tensor(best[:, s % 2, :], cost[:, s, 0:BR], cost[:, s, 1:BR + 1], ALU.min).then_inc(s_v, 1)
                done[0] += 2
                halo = done[0]
                g, k = s // GC * GC - GC, s % GC
                if g >= 0 and k:
                    dve.wait_ge(s_v, made[2 * k - 1])
                if g >= 0:
                    made[2 * k] = choice(g, 2 * k)
                dve.wait_ge(s_v, halo)
                nc.vector.tensor_tensor_scan(cost[:, s + 1, 1:BR + 1], best[:, s % 2, :], big[:, :, s],
                                             cost[:, s + 1, 0:1], ALU.min, ALU.add).then_inc(s_v, 1)
                done[0] += 1
                cell = done[0]
                if g >= 0 and k < GC - 1:
                    if k:
                        dve.wait_ge(s_v, made[2 * k])
                    made[2 * k + 1] = choice(g, 2 * k + 1)
                dve.wait_ge(s_v, cell)
            for k in range(5):
                made[k] = choice(W - GC, k)
                dve.wait_ge(s_v, made[k])
            dve.wait_ge(s_pool, POOL_ALL)
            down = [(p & 16) | min((p & 15) + 1, 15) for p in range(32)]
            for m in (ups, goes):
                link(nc.vector.stream_shuffle(m[:, 0:W - 1, 0, 0], m[:, 1:W, BR, 0], down))
            step0 = step_in[:, 0, :]
            nc.vector.memset(trail[:, W - 1, 0:1], 0.0)
            link(nc.vector.tensor_copy(step0, seed[:, :]))
            for s in reversed(range(W)):
                if s < W - 1:
                    nc.vector.stream_shuffle(trail[:, s, 0:1], trail[:, s + 1, 2 * BR:2 * BR + 1], down).then_inc(s_v, 1)
                    t = trail[:, s + 1, 0:2]
                    pair = bass.AP(tensor=t.tensor, offset=t.offset, ap=[list(t.ap[0]), [2, BR], [2, 2]])
                    nc.vector.tensor_tensor(step0.rearrange("p (r t) -> p r t", t=2), pair,
                                            goes[:, s + 1, 0:BR, :], ALU.mult).then_inc(s_v, 1)
                    done[0] += 2
                    dve.wait_ge(s_v, done[0])
                nc.vector.tensor_tensor_scan(trail[:, s, 1:2 * BR + 1],
                                             ups[:, s, 0:BR, :].rearrange("p r t -> p (r t)"), step0,
                                             trail[:, s, 0:1], ALU.mult, ALU.add).then_inc(s_back, 1)
                dve.wait_ge(s_back, W - s)

            def two(a, g):
                return a[0:J, 2 * g:2 * g + 2, :]

            def pair(i):
                return bank[i][0:J, :].rearrange("p (b h) -> p b h", b=2)

            for turn in range(PG + 4):
                g0, g1, g2, g3, g4 = (turn - n for n in LAG)
                if g0 < PG:
                    dve.wait_ge(s_exp, g0 + 1)
                    nc.vector.tensor_tensor(two(xs, g0), two(xs, g0), pair(4 + g0), ALU.add).then_inc(s_x2, 1)
                for n, g in ((0, g1), (1, g2), (2, g4)):
                    if 0 <= g < PG:
                        dve.wait_ge(s_dev[n], g + 1)
                        last = nc.vector.reciprocal(rstd[0:J, n, 2 * g:2 * g + 2], std[0:J, n, 2 * g:2 * g + 2])
                if turn:
                    link(last)
                for n, g in ((1, g2), (2, g4)):
                    if 0 <= g < PG:
                        dve.wait_ge(s_mv[n], g + 1)
                        nc.vector.scalar_tensor_tensor(shift[0:J, n, 2 * g:2 * g + 2], mv[0:J, n, 2 * g:2 * g + 2, 0], -1.0,
                                                       rstd[0:J, n, 2 * g:2 * g + 2], ALU.mult, ALU.mult
                                                       ).then_inc(s_scale[n], 1)
                if 0 <= g1 < PG:
                    dve.wait_ge(s_mv[0], g1 + 1)
                    for b in (2 * g1, 2 * g1 + 1):
                        nc.vector.tensor_scalar(xn[0:J, b, :], xs[0:J, b, :], mv[0:J, 0, b, 0:1], rstd[0:J, 0, b:b + 1],
                                                ALU.subtract, ALU.mult).then_inc(s_y, 1)
                if g0 < PG:
                    dve.wait_ge(s_x2, g0 + 1)
                    for b in (2 * g0, 2 * g0 + 1):
                        last = nc.vector.bn_stats(out=bn6[0:J, 0, b, :], in_=xs[0:J, b, :])
                if 0 <= g3 < PG:
                    dve.wait_ge(s_att, g3 + 1)
                    dve.wait_ge(s_exp, PG)
                    nc.vector.tensor_tensor(two(hs, g3), two(xn, g3), pair(4 + g3 % 2), ALU.add).then_inc(s_h, 1)
                if 0 <= g1 < PG:
                    dve.wait_ge(s_y, 2 * g1 + 2)
                    for b in (2 * g1, 2 * g1 + 1):
                        last = nc.vector.bn_stats(out=bn6[0:J, 1, b, :], in_=xn[0:J, b, :])
                if 0 <= g3 < PG:
                    dve.wait_ge(s_h, g3 + 1)
                    for b in (2 * g3, 2 * g3 + 1):
                        last = nc.vector.bn_stats(out=bn6[0:J, 2, b, :], in_=hs[0:J, b, :])
                if turn < PG + 3:
                    link(last)
                for n, g in ((0, g0), (1, g1), (2, g3)):
                    if 0 <= g < PG:
                        for b in (2 * g, 2 * g + 1):
                            last = nc.vector.bn_aggr(out=mv[0:J, n, b, :], in_=bn6[0:J, n, b, :])
                        last.then_inc(s_mv[n], 1)

            dve.wait_ge(s_log, PG)
            logit = bank[6][0:J, 0:NB * NE].rearrange("p (b e) -> p b e", b=NB)
            for b in range(NB):
                last = nc.vector.max(out=top[0:J, b, :], in_=logit[:, b, :])
            link(last)
            for b in range(NB):
                nc.vector.max_index(out=topi[0:J, b, :], in_max=top[0:J, b, :], in_values=logit[:, b, :])
            nc.vector.tensor_tensor(tops[0:J, :, 0], top[0:J, :, 0], top[0:J, :, 1], ALU.subtract)
            nc.vector.tensor_tensor(tops[0:J, :, 1], top[0:J, :, 1], top[0:J, :, 0], ALU.subtract).then_inc(s_dif, 1)
            dve.wait_ge(s_dif, 1)
            for k in range(TOP):
                last = nc.vector.tensor_tensor(picked[0:J, k, :, :], iota_e[0:J, :].unsqueeze(1).to_broadcast([J, NB, NE]),
                                               topi[0:J, :, k:k + 1].to_broadcast([J, NB, NE]), ALU.is_equal)
            link(last)
            nc.vector.tensor_tensor(chosen[0:J, :, :], picked[0:J, 0, :, :], picked[0:J, 1, :, :],
                                    ALU.add).then_inc(s_pick, 1)
            dve.wait_ge(s_sig, 1)
            link(nc.vector.tensor_copy(w_part[0:J, 0, :, :], tops[0:J, :, :]))
            link(nc.vector.tensor_tensor(w_rest[0:J, :, :], tops[0:J, :, :], w_part[0:J, 0, :, :], ALU.subtract))
            link(nc.vector.tensor_copy(w_part[0:J, 1, :, :], w_rest[0:J, :, :]))
            nc.vector.tensor_tensor(w_part[0:J, 2, :, :], w_rest[0:J, :, :], w_part[0:J, 1, :, :], ALU.subtract)
            dve.wait_ge(s_rank, 1)
            link(nc.vector.tensor_copy(count[:, :], bank[7][:, NB * NE:NB * NE + NE]))
            link(nc.vector.tensor_tensor(more[:, :, :], count[:, :].unsqueeze(2).to_broadcast([128, NE, MT]),
                                         steps[:, :].unsqueeze(1).to_broadcast([128, NE, MT]), ALU.is_gt))
            link(nc.vector.tensor_reduce(tiles[:, :], more[:, :, :], AX_X, ALU.add))
            link(nc.vector.tensor_tensor_scan(ends[:, :], tiles[:, :], zero8[:, :], 0.0, ALU.add, ALU.add))
            link(nc.vector.tensor_tensor(base[:, :], ends[:, :], tiles[:, :], ALU.subtract))
            link(nc.vector.scalar_tensor_tensor(place[0:J, :, :], base[0:J, :].unsqueeze(1).to_broadcast([J, NB, NE]),
                                                float(ST), bank[7][0:J, 0:NB * NE].rearrange("p (b e) -> p b e", b=NB),
                                                ALU.mult, ALU.add))
            for k in range(TOP):
                last = nc.vector.tensor_tensor(hit[0:J, k, :, :], picked[0:J, k, :, :], place[0:J, :, :], ALU.mult)
            link(last)
            link(nc.vector.tensor_reduce(placef[0:J, :, :], hit[0:J, :, :, :], AX_X, ALU.add))
            link(nc.vector.tensor_copy(slot[0:J, :, :], placef[0:J, :, :]))
            link(nc.vector.tensor_scalar(inner[0:J, :, :], slot[0:J, :, :], ST - 1, None, ALU.bitwise_and))
            link(nc.vector.tensor_tensor(outer[0:J, :, :], slot[0:J, :, :], inner[0:J, :, :], ALU.subtract))
            n = TOP * NB
            outer_b = outer[0:J, :, :].rearrange("p k b -> p (k b)").unsqueeze(2).to_broadcast([J, n, NT])
            link(nc.vector.tensor_tensor(in_tile[0:J, :, :], outer_b,
                                         tile_first[0:J, :].unsqueeze(1).to_broadcast([J, n, NT]), ALU.is_equal))
            for k in range(TOP):
                o = slice(k * NB, (k + 1) * NB)
                nc.vector.tensor_tensor(marks[0:J, o, 0, :], in_tile[0:J, o, :],
                                        batch_at[0:J, :].unsqueeze(2).to_broadcast([J, NB, NT]), ALU.mult)
            nc.vector.tensor_scalar(marks[0:J, :, 1, :], in_tile[0:J, :, :], row_at[0:J, :], None, ALU.mult)
            for q in range(0, n, 4):
                nc.vector.tensor_tensor(match[0:J, q:q + 4, :],
                                        inner[0:J, :, :].rearrange("p k b -> p (k b)")[:, q:q + 4]
                                        .unsqueeze(2).to_broadcast([J, 4, ST]),
                                        row_no[0:J, :].unsqueeze(1).to_broadcast([J, 4, ST]),
                                        ALU.is_equal).then_inc(s_match, 1)
            dve.wait_ge(s_marks, 1)
            link(nc.vector.tensor_copy(part[:, 0:2, :], bank[0][:, 0:2 * NT].rearrange("p (k t) -> p k t", k=2)))
            link(nc.vector.tensor_tensor(slot_t[:, :], part[:, 0, :], part[:, 1, :], ALU.add))
            nc.vector.tensor_scalar(fetch[:, :], slot_t[:, :], 1.0, 0.0, ALU.subtract, ALU.max).then_inc(s_index, 1)
            nc.vector.tensor_scalar(empty[:, :], slot_t[:, :], 0.0, behind[:, :], ALU.is_equal, ALU.mult)
            for k in range(TOP):
                o = slice(k * NB, (k + 1) * NB)
                for m in range(3):
                    last = nc.vector.tensor_tensor(marks[0:J, o, 2 + m, :], in_tile[0:J, o, :],
                                                   w_part[0:J, m, :, k:k + 1].to_broadcast([J, NB, NT]), ALU.mult)
            last.then_inc(s_heavy, 1)
            dve.wait_ge(s_heavy, 1)
            nc.vector.scalar_tensor_tensor(target[:, :], empty[:, :], 1.0, slot_t[:, :],
                                           ALU.subtract, ALU.add).then_inc(s_index, 1)
            link(nc.vector.tensor_tensor(passed[:, :, :], ends[:, :].unsqueeze(1).to_broadcast([128, NT, NE]),
                                         tile_no[:, :].unsqueeze(2).to_broadcast([128, NT, NE]), ALU.is_le))
            link(nc.vector.tensor_reduce(tile_e[:, :], passed[:, :, :], AX_X, ALU.add))
            link(nc.vector.tensor_scalar(tile_e[:, :], tile_e[:, :], float(NE - 1), None, ALU.min))
            nc.vector.tensor_scalar(wrap[:, 0, :], tile_e[:, :], float(RING), -float(RING), ALU.is_ge, ALU.mult)
            link(nc.vector.tensor_scalar(wrap[:, 1, :], tile_e[:, :], float(2 * RING), -float(RING), ALU.is_ge, ALU.mult))
            link(nc.vector.tensor_tensor(wrap[:, 0, :], wrap[:, 0, :], wrap[:, 1, :], ALU.add))
            link(nc.vector.tensor_tensor(tile_w[:, :], wrap[:, 0, :], tile_e[:, :], ALU.add))
            nc.vector.tensor_scalar(table[:, 1, :], tile_w[0:1, :], float(EW), None, ALU.mult)
            nc.vector.tensor_copy(table[:, 0, :], tile_e[0:1, :])
            nc.vector.tensor_copy(ends_i[:, :], ends[0:1, :]).then_inc(s_table, 1)
            dve.wait_ge(s_marks, 2)
            link(nc.vector.tensor_copy(part[:, 2:5, :], bank[1][:, 0:3 * NT].rearrange("p (k t) -> p k t", k=3)))
            link(nc.vector.tensor_tensor(slot_w[:, :], part[:, 2, :], part[:, 3, :], ALU.add))
            nc.vector.tensor_tensor(slot_w[:, :], slot_w[:, :], part[:, 4, :], ALU.add).then_inc(s_table, 1)
            dve.wait_ge(s_table, 2)

            def inputs(t, p):
                dve.wait_ge(s_in_t, t + 1)
                if not isinstance(t, int) or t >= 2:
                    dve.wait_ge(s_gu, 2 * t - 2)
                for c in range(HC):
                    last = nc.vector.tensor_scalar(tT[:, p, c, :], bank[7][:, c * ST:(c + 1) * ST],
                                                   ln_w[:, 2, c:c + 1], ln_w[:, 3, c:c + 1], ALU.mult, ALU.add)
                last.then_inc(s_in, 1)

            def hidden(n, q):
                dve.wait_ge(s_silu, n + 1)
                if not isinstance(n, int) or n >= 2:
                    dve.wait_ge(s_ht, n - 1)
                nc.vector.tensor_tensor(hid[:, q, :], act_g[:, q, :], bank[2 + q][:, :], ALU.mult).then_inc(s_hid, 1)

            def scale(t, p):
                dve.wait_ge(s_down, 2 * t + 3)
                if not isinstance(t, int) or t >= 2:
                    dve.wait_ge(s_added, 16 * (t - 1))
                nc.vector.tensor_scalar(scaled[:, p, :], bank[6][:, 0:H], slot_w[:, bass.ds(t, 1)], None,
                                        ALU.mult).then_inc(s_o, 1)

            used = dve.value_load(ends_i[0:1, NE - 1:NE], min_val=NE, max_val=NT)
            inputs(0, 0)
            hidden(0, 0)
            inputs(1, 1)
            hidden(1, 1)
            hidden(2, 0)

            def whole_tile(t, p):
                inputs(t + 1, 1 - p)
                hidden(2 * t + 1, 1)
                scale(t - 1, 1 - p)
                hidden(2 * t + 2, 0)

            def tile(t, p):
                with dve.If(t < used):
                    with dve.If(t + 1 < used):
                        inputs(t + 1, 1 - p)
                    hidden(2 * t + 1, 1)
                    scale(t - 1, 1 - p)
                    with dve.If(t + 1 < used):
                        hidden(2 * t + 2, 0)
                with dve.Else():
                    with dve.If(t - 1 < used):
                        scale(t - 1, 1 - p)

            whole_tile(1, 1)
            whole_tile(2, 0)
            with dve.Fori(1, (NT - 2) // 2) as i:
                tile(2 * i + 1, 1)
                tile(2 * i + 2, 0)
            with dve.If(used > NT - 1):
                hidden(2 * NT - 1, 1)
                scale(NT - 2, 0)
                scale(NT - 1, 1)
            with dve.Else():
                with dve.If(used > NT - 2):
                    scale(NT - 2, 0)

        @block.tensor
        def _(pe):
            pe.wait_ge(s_pool, POOL_FIRST)
            for h in range(2):
                for c in range(HC):
                    for b in range(G * h, G * h + G):
                        pe.wait_ge(s_norm, b + 1)
                        last = nc.tensor.transpose(bank[2 * c + h][:, (b % G) * J:(b % G + 1) * J],
                                                   xn[0:J, b, c * 128:(c + 1) * 128], ident[0:J, 0:J])
                    last.then_inc(s_tr, 1)
            for n in range(2 * NC):
                c, h = n // 2, n % 2
                if h == 0:
                    pe.wait_ge(s_ct[c], 16)
                pe.wait_ge(s_trc, HC * h + HC)
                if n >= 6:
                    pe.wait_ge(s_sqd, n - 5)
                for b in range(G * h, G * h + G):
                    o = bank[D_BANK[n % 6]][0:ROWS[c], (b % G) * J:(b % G + 1) * J]
                    for kc in range(HC):
                        last = nc.tensor.matmul(o, ctxT[c][:, kc, b, :], xT[:, kc, b, :],
                                                start=(kc == 0), stop=(kc == HC - 1))
                last.then_inc(s_dot, 1)
                if c == 0:
                    pe.wait_ge(s_xsq, HC * h + HC)
                    for kc in range(HC):
                        last = nc.tensor.matmul(bank[h][0:CR, 0:G * J], quarter[:, :],
                                                xsq[:, kc, G * h:G * h + G, :].rearrange("p b j -> p (b j)"),
                                                start=(kc == 0), stop=(kc == HC - 1))
                    last.then_inc(s_bb, 1)

            def keep_awake(n):
                for _ in range(n):
                    nc.tensor.matmul(bank[3][:, 0:256], ident[:, :], attn_w[:, 0, :], start=True, stop=True)

            pe.wait_ge(s_small, 48)
            pe.wait_ge(s_path, len(COPIES) - NC + 2)
            keep_awake(9)
            for c in reversed(range(NC)):
                pe.wait_ge(s_unskew[c], 16)
                for b in range(NB):
                    last = nc.tensor.matmul(bank[4 + b // 2][0:J, b % 2 * H:(b % 2 + 1) * H],
                                            stage[0:ROWS[c], c, b, :], ctxn[0:ROWS[c], c, b, :],
                                            start=(c == NC - 1 and b % 2 == 0), stop=(c == 0 and b % 2 == 1))
                    if c == 0 and b % 2:
                        last.then_inc(s_exp, 1)

            def turn_pair(g, first_bank, ready, turned, copied):
                pe.wait_ge(ready, g + 1)
                if g >= 2:
                    pe.wait_ge(copied, g - 1)
                for c in range(HC):
                    for b in range(2):
                        o = (2 * c + b) * J
                        last = nc.tensor.transpose(bank[first_bank + g % 2][:, o:o + J],
                                                   zs[0:J, 2 * g + b, c * 128:(c + 1) * 128], ident[0:J, 0:J])
                last.then_inc(turned, 1)

            keep_awake(8)
            for turn in range(2, PG + 4):
                g2, g3 = turn - 2, turn - 4
                if g2 < PG:
                    turn_pair(g2, 0, s_z, s_zt, s_ztc)
                if 0 <= g3:
                    turn_pair(g3, 2, s_t, s_tt, s_ttc)
                if g2 < PG:
                    pe.wait_ge(s_ztc, g2 + 1)
                    pe.wait_ge(s_x2, min(g2 + 1, 2))
                    if g2 >= 2:
                        pe.wait_ge(s_h, g2 - 1)
                    for b in range(2):
                        for c in range(HC):
                            last = nc.tensor.matmul(bank[4 + g2 % 2][0:J, b * H:(b + 1) * H], xT[:, c, 2 * g2 + b, :],
                                                    attn_w[:, c, :], start=(c == 0), stop=(c == HC - 1))
                    last.then_inc(s_att, 1)
                if 0 <= g3:
                    pe.wait_ge(s_ttc, g3 + 1)
                    if g3 == 0:
                        pe.wait_ge(s_x2, PG)
                    for b in (2 * g3, 2 * g3 + 1):
                        for c in range(HC):
                            last = nc.tensor.matmul(bank[6][0:J, b * NE:(b + 1) * NE], xT[:, c, b, :], gate_w[:, c, :],
                                                    start=(c == 0), stop=(c == HC - 1))
                    last.then_inc(s_log, 1)

            pe.wait_ge(s_pick, 1)
            chosen_f = chosen[0:J, :, :].rearrange("p b e -> p (b e)")
            nc.tensor.matmul(bank[7][0:J, 0:NB * NE], before[0:J, 0:J], chosen_f, start=True, stop=False)
            for d in range(1, NB):
                nc.tensor.matmul(bank[7][0:J, d * NE:NB * NE], ones[0:J, 0:J], chosen_f[:, 0:(NB - d) * NE],
                                 start=False, stop=(d == NB - 1))
            for b in range(NB):
                last = nc.tensor.matmul(bank[7][:, NB * NE:NB * NE + NE], ones[0:J, :], chosen_f[:, b * NE:(b + 1) * NE],
                                        start=(b == 0), stop=(b == NB - 1))
            last.then_inc(s_rank, 1)
            n = TOP * NB
            for i in range(n):
                pe.wait_ge(s_match, i // 4 + 1)
                last = nc.tensor.matmul(bank[0][:, 0:2 * NT], match[0:J, i, :],
                                        marks[0:J, i, 0:2, :].rearrange("p k t -> p (k t)"),
                                        start=(i == 0), stop=(i == n - 1))
            last.then_inc(s_marks, 1)
            keep_awake(5)
            pe.wait_ge(s_heavy, 1)
            for i in range(n):
                last = nc.tensor.matmul(bank[1][:, 0:3 * NT], match[0:J, i, :],
                                        marks[0:J, i, 2:5, :].rearrange("p k t -> p (k t)"),
                                        start=(i == 0), stop=(i == n - 1))
            last.then_inc(s_marks, 1)
            pe.wait_ge(s_index, 1)
            pe.wait_ge(s_table, 2)
            pe.sem_inc(s_down, 1)

            def expert(t):
                return pe.value_load(table[0:1, 0, bass.ds(t, 1)], min_val=0, max_val=NE - 1)

            def place_of(t):
                return pe.value_load(table[0:1, 1, bass.ds(t, 1)], min_val=0, max_val=(RING - 1) * EW)

            def turn_in(t, p, loads):
                pe.wait_ge(s_row[p], 16 * loads)
                if not isinstance(t, int) or t >= 1:
                    pe.wait_ge(s_in, t)
                for c in range(HC):
                    last = nc.tensor.transpose(bank[7][:, c * ST:(c + 1) * ST],
                                               row_in[:, p, c * 128:(c + 1) * 128],
                                               ident[:, :])
                last.then_inc(s_in_t, 1)

            def gate_up(n, q, p, at):
                if not isinstance(n, int) or n >= 2:
                    pe.wait_ge(s_hid, n - 1)
                for k in range(2):
                    for c in range(HC):
                        nc_o = (k * HC + c) * F + q * 512
                        last = nc.tensor.matmul(bank[2 * k + q][:, :], tT[:, p, c, :], wflat[:, bass.ds(at + nc_o, 512)],
                                                start=(c == 0), stop=(c == HC - 1))
                last.then_inc(s_gu, 1)

            def first_half(t, p):
                e, at = expert(t), place_of(t)
                pe.wait_ge(s_ready, e + 1)
                pe.wait_ge(s_in, t + 1)
                gate_up(2 * t, 0, p, at)

            def turn_hidden(n, q):
                pe.wait_ge(s_hid, n + 1)
                if not isinstance(n, int) or n >= 2:
                    pe.wait_ge(s_htc, n - 1)
                for f in range(4):
                    last = nc.tensor.transpose(bank[4 + q][:, f * ST:(f + 1) * ST], hid[:, q, f * 128:(f + 1) * 128],
                                               ident[:, :])
                last.then_inc(s_ht, 1)

            def down(n, q, t, p, at):
                pe.wait_ge(s_htc, n + 1)
                if q == 0 and (not isinstance(t, int) or t >= 1):
                    pe.wait_ge(s_o, t)
                for f in range(4):
                    o = 2 * HC * F + (4 * q + f) * H
                    last = nc.tensor.matmul(bank[6][:, 0:H], hidT[:, q, f, :],
                                            wflat[:, bass.ds(at + o, H)], start=(q == 0 and f == 0), stop=(q == 1 and f == 3))
                last.then_inc(s_down, 1)

            used = pe.value_load(ends_i[0:1, NE - 1:NE], min_val=NE, max_val=NT)

            def tile(t, p, loads):
                with pe.If(t < used):
                    here = place_of(t)
                    gate_up(2 * t + 1, 1, p, here)
                    with pe.If(t + 1 < used):
                        turn_in(t + 1, 1 - p, loads)
                    turn_hidden(2 * t, 0)
                    down(2 * t - 1, 1, t - 1, 1 - p, place_of(t - 1))
                    with pe.If(t + 1 < used):
                        first_half(t + 1, 1 - p)
                    turn_hidden(2 * t + 1, 1)
                    down(2 * t, 0, t, p, here)
                with pe.Else():
                    with pe.If(t - 1 < used):
                        down(2 * t - 1, 1, t - 1, 1 - p, place_of(t - 1))

            keep_awake(2)
            turn_in(0, 0, 1)
            first_half(0, 0)
            here = place_of(0)
            gate_up(1, 1, 0, here)
            turn_in(1, 1, 1)
            turn_hidden(0, 0)
            first_half(1, 1)
            turn_hidden(1, 1)
            down(0, 0, 0, 0, here)
            with pe.Fori(0, (NT - 2) // 2) as i:
                tile(2 * i + 1, 1, i + 2)
                tile(2 * i + 2, 0, i + 2)
            with pe.If(used > NT - 1):
                here = place_of(NT - 1)
                gate_up(2 * NT - 1, 1, 1, here)
                turn_hidden(2 * NT - 2, 0)
                down(2 * NT - 3, 1, NT - 2, 0, place_of(NT - 2))
                turn_hidden(2 * NT - 1, 1)
                down(2 * NT - 2, 0, NT - 1, 1, here)
                down(2 * NT - 1, 1, NT - 1, 1, here)
            with pe.Else():
                with pe.If(used > NT - 2):
                    down(2 * NT - 3, 1, NT - 2, 0, place_of(NT - 2))


def kernel(x, ctx_1024, L0_ffn_ln1_g, L0_ffn_ln1_b, L0_ffn_attn_w, L0_ffn_ln2_g, L0_ffn_ln2_b,
           L0_ffn_gate_w, L0_ffn_gate_proj, L0_ffn_up_proj, L0_ffn_down_proj):
    import numpy as np
    import concourse.bacc as bacc
    from concourse.bass_utils import run_bass_kernel_spmd

    def by_partition(a, axis):
        a = np.moveaxis(np.asarray(a), axis, 0)
        return np.moveaxis(a.reshape((a.shape[0] // 128, 128) + a.shape[1:]), 0, 1)

    ctx = np.asarray(ctx_1024)
    ln = np.stack([np.asarray(v) for v in (L0_ffn_ln1_g, L0_ffn_ln1_b, L0_ffn_ln2_g, L0_ffn_ln2_b)])
    laid = {
        "x": np.asarray(x).transpose(1, 0, 2),
        "ctx_t": np.concatenate([by_partition(ctx[:, c * CR:c * CR + ROWS[c]], 2).reshape(128, -1) for c in range(NC)], 1),
        "ctx_n": ctx.transpose(1, 0, 2),
        "ln": by_partition(ln, 1).transpose(0, 2, 1),
        "attn_t": by_partition(L0_ffn_attn_w, 1),
        "gate_t": by_partition(L0_ffn_gate_w, 1),
        "gate_proj": np.stack([by_partition(w, 1) for w in np.asarray(L0_ffn_gate_proj)]).reshape(NE, 128, HC * F),
        "up_proj": np.stack([by_partition(w, 1) for w in np.asarray(L0_ffn_up_proj)]).reshape(NE, 128, HC * F),
        "down_proj": np.stack([by_partition(w, 1) for w in np.asarray(L0_ffn_down_proj)]).reshape(NE, 128, FC * H),
    }
    nc = bacc.Bacc("TRN2", target_bir_lowering=False, num_devices=1)
    arrays, args = {}, []
    for name, a in laid.items():
        arrays[name] = np.ascontiguousarray(a)
        args.append(nc.dram_tensor(name, a.shape, mybir.dt.from_np(a.dtype), kind="ExternalInput").ap())
    args.append(nc.dram_tensor("out", (NB * J + ST, H), F32, kind="ExternalOutput").ap())
    align_and_route(nc, *args)
    got = run_bass_kernel_spmd(nc, [arrays], core_ids=[0]).results[0]["out"]
    return np.ascontiguousarray(got[0:NB * J].reshape(NB, J, H))
```
